# Optimizing a Trainium2 kernel written in Bass

```python
import numpy as np
import jax
import jax.numpy as jnp

def _softmax(x, axis=-1):
    return jax.nn.softmax(x, axis=axis)

def _gelu(x):
    return jax.nn.gelu(x, approximate=True)

def _silu(x):
    return jax.nn.silu(x)

def _sigmoid(x):
    return jax.nn.sigmoid(x)

def _layernorm(x, axis=-1, eps=1e-05):
    m = jnp.mean(x, axis=axis, keepdims=True)
    v = jnp.var(x, axis=axis, keepdims=True)
    return (x - m) / jnp.sqrt(v + eps)

def _scatter_add(tgt, idx, src, axis=0):
    return tgt.at[idx].add(src)

def _segment_sum(src, seg, n):
    return jax.ops.segment_sum(src, seg, n)
kernel_name = 'mk_macaron_d1_jaxref_r4_4d12ae'

def setup_inputs(seed: int=0):
    np.random.seed(seed)
    _w = jnp.asarray

    def _L0_attn_setup():
        import jax, jax.numpy as jnp
        from jax import lax
        import numpy as np
        HEAD_SIZE = 64
        D_MIX = 32
        D_DECAY = 64
        D_GATE = 64

        def _wkv6(r, k, v, w, u):
            B, T, C = r.shape
            N = HEAD_SIZE
            H = C // N
            to_h = lambda a: a.reshape(B, T, H, N).transpose(1, 0, 2, 3)
            rT, kT, vT, wT = map(to_h, (r, k, v, w))

            def step(S, inp):
                rt, kt, vt, wt = inp
                kv = kt[..., :, None] * vt[..., None, :]
                y = jnp.einsum('bhi,bhij->bhj', rt, S + u[None, :, :, None] * kv)
                S = wt[..., None] * S + kv
                return (S, y)
            S0 = jnp.zeros((B, H, N, N), r.dtype)
            _, y = lax.scan(step, S0, (rT, kT, vT, wT))
            return y.transpose(1, 0, 2, 3).reshape(B, T, C)
        key = jax.random.key(seed)
        B, T, C = (4, 512, 256)
        H = C // HEAD_SIZE
        ks = jax.random.split(key, 24)
        n = lambda i, shape, s=1.0: jax.random.normal(ks[i], shape, dtype=jnp.float32) * s
        return {'x': n(0, (B, T, C)), 'maa_x': n(1, (C,), 0.1), 'maa_w': n(2, (C,), 0.1), 'maa_k': n(3, (C,), 0.1), 'maa_v': n(4, (C,), 0.1), 'maa_r': n(5, (C,), 0.1), 'maa_g': n(6, (C,), 0.1), 'maa_w1': n(7, (C, 5 * D_MIX), 0.01), 'maa_w2': n(8, (5, D_MIX, C), 0.01), 'Wr': n(9, (C, C), C ** (-0.5)), 'Wk': n(10, (C, C), C ** (-0.5)), 'Wv': n(11, (C, C), C ** (-0.5)), 'Wo': n(12, (C, C), C ** (-0.5)), 'gate_w1': n(13, (C, D_GATE), 0.01), 'gate_w2': n(14, (D_GATE, C), 0.01), 'time_decay': n(15, (C,), 1.0) - 4.0, 'decay_w1': n(16, (C, D_DECAY), 0.01), 'decay_w2': n(17, (D_DECAY, C), 0.01), 'u': n(18, (H, HEAD_SIZE), 0.1), 'ln_g': jnp.ones((C,), jnp.float32), 'ln_b': jnp.zeros((C,), jnp.float32)}
    _L0_attn_in = _L0_attn_setup()

    def _L0_ffn_setup():
        import math
        import jax, jax.numpy as jnp
        import numpy as np
        NUM_EXPERTS = 16
        TOP_K = 2
        CAPACITY_FACTOR = 1.25
        key = jax.random.key(seed)
        k1, k2, k3, k4 = jax.random.split(key, 4)
        d, dff, E = (256, 1024, NUM_EXPERTS)
        x = jax.random.normal(k1, (4, 512, d), dtype=jnp.float32)
        router_w = jax.random.normal(k2, (E, d), dtype=jnp.float32) * d ** (-0.5)
        router_b = jnp.zeros((E,), dtype=jnp.float32)
        w1 = jax.random.normal(k3, (E, d, dff), dtype=jnp.float32) * 0.02
        b1 = jnp.zeros((E, dff), dtype=jnp.float32)
        w2 = jax.random.normal(k4, (E, dff, d), dtype=jnp.float32) * 0.02
        b2 = jnp.zeros((E, d), dtype=jnp.float32)
        return {'x': x, 'router_w': router_w, 'router_b': router_b, 'w1': w1, 'b1': b1, 'w2': w2, 'b2': b2}
    _L0_ffn_in = _L0_ffn_setup()
    _d = {'L0_attn_x': _L0_attn_in['x'], 'L0_attn_maa_x': _L0_attn_in['maa_x'], 'L0_attn_maa_w': _L0_attn_in['maa_w'], 'L0_attn_maa_k': _L0_attn_in['maa_k'], 'L0_attn_maa_v': _L0_attn_in['maa_v'], 'L0_attn_maa_r': _L0_attn_in['maa_r'], 'L0_attn_maa_g': _L0_attn_in['maa_g'], 'L0_attn_maa_w1': _L0_attn_in['maa_w1'], 'L0_attn_maa_w2': _L0_attn_in['maa_w2'], 'L0_attn_Wr': _L0_attn_in['Wr'], 'L0_attn_Wk': _L0_attn_in['Wk'], 'L0_attn_Wv': _L0_attn_in['Wv'], 'L0_attn_Wo': _L0_attn_in['Wo'], 'L0_attn_gate_w1': _L0_attn_in['gate_w1'], 'L0_attn_gate_w2': _L0_attn_in['gate_w2'], 'L0_attn_time_decay': _L0_attn_in['time_decay'], 'L0_attn_decay_w1': _L0_attn_in['decay_w1'], 'L0_attn_decay_w2': _L0_attn_in['decay_w2'], 'L0_attn_u': _L0_attn_in['u'], 'L0_attn_ln_g': _L0_attn_in['ln_g'], 'L0_attn_ln_b': _L0_attn_in['ln_b'], 'L0_ffn_router_w': _L0_ffn_in['router_w'], 'L0_ffn_router_b': _L0_ffn_in['router_b'], 'L0_ffn_w1': _L0_ffn_in['w1'], 'L0_ffn_b1': _L0_ffn_in['b1'], 'L0_ffn_w2': _L0_ffn_in['w2'], 'L0_ffn_b2': _L0_ffn_in['b2']}
    _x0 = _d['L0_attn_x']
    _d['L0_attn_x'] = jax.random.normal(jax.random.fold_in(jax.random.key(seed), 1), (8, 1024, 256), dtype=_x0.dtype)
    del _x0
    return _d

def reference(L0_attn_x, L0_attn_maa_x, L0_attn_maa_w, L0_attn_maa_k, L0_attn_maa_v, L0_attn_maa_r, L0_attn_maa_g, L0_attn_maa_w1, L0_attn_maa_w2, L0_attn_Wr, L0_attn_Wk, L0_attn_Wv, L0_attn_Wo, L0_attn_gate_w1, L0_attn_gate_w2, L0_attn_time_decay, L0_attn_decay_w1, L0_attn_decay_w2, L0_attn_u, L0_attn_ln_g, L0_attn_ln_b, L0_ffn_router_w, L0_ffn_router_b, L0_ffn_w1, L0_ffn_b1, L0_ffn_w2, L0_ffn_b2):

    def _L0_attn_ref(x, maa_x, maa_w, maa_k, maa_v, maa_r, maa_g, maa_w1, maa_w2, Wr, Wk, Wv, Wo, gate_w1, gate_w2, time_decay, decay_w1, decay_w2, u, ln_g, ln_b):
        import jax, jax.numpy as jnp
        from jax import lax
        import numpy as np
        HEAD_SIZE = 64
        D_MIX = 32
        D_DECAY = 64
        D_GATE = 64

        def _wkv6(r, k, v, w, u):
            B, T, C = r.shape
            N = HEAD_SIZE
            H = C // N
            to_h = lambda a: a.reshape(B, T, H, N).transpose(1, 0, 2, 3)
            rT, kT, vT, wT = map(to_h, (r, k, v, w))

            def step(S, inp):
                rt, kt, vt, wt = inp
                kv = kt[..., :, None] * vt[..., None, :]
                y = jnp.einsum('bhi,bhij->bhj', rt, S + u[None, :, :, None] * kv)
                S = wt[..., None] * S + kv
                return (S, y)
            S0 = jnp.zeros((B, H, N, N), r.dtype)
            _, y = lax.scan(step, S0, (rT, kT, vT, wT))
            return y.transpose(1, 0, 2, 3).reshape(B, T, C)
        B, T, C = x.shape
        H, N = (C // HEAD_SIZE, HEAD_SIZE)
        xx = jnp.concatenate([jnp.zeros_like(x[:, :1]), x[:, :-1]], axis=1) - x
        xxx = x + xx * maa_x
        lora = jnp.tanh(xxx @ maa_w1).reshape(B, T, 5, D_MIX)
        m = jnp.einsum('btfd,fdc->fbtc', lora, maa_w2)
        mw, mk, mv, mr, mg = (m[0], m[1], m[2], m[3], m[4])
        xw = x + xx * (maa_w + mw)
        xk = x + xx * (maa_k + mk)
        xv = x + xx * (maa_v + mv)
        xr = x + xx * (maa_r + mr)
        xg = x + xx * (maa_g + mg)
        r = xr @ Wr
        k = xk @ Wk
        v = xv @ Wv
        g = jnp.tanh(xg @ gate_w1) @ gate_w2
        w = time_decay + jnp.tanh(xw @ decay_w1) @ decay_w2
        wdec = jnp.exp(-jnp.exp(w))
        y = _wkv6(r, k, v, wdec, u)
        yh = y.reshape(B, T, H, N)
        mu = yh.mean(-1, keepdims=True)
        var = yh.var(-1, keepdims=True)
        yn = ((yh - mu) / jnp.sqrt(var + 0.00064)).reshape(B, T, C) * ln_g + ln_b
        return yn * g @ Wo

    def _L0_ffn_ref(x, router_w, router_b, w1, b1, w2, b2):
        import math
        import jax, jax.numpy as jnp
        import numpy as np
        NUM_EXPERTS = 16
        TOP_K = 2
        CAPACITY_FACTOR = 1.25
        E, k = (NUM_EXPERTS, TOP_K)
        B, S, d = x.shape
        tokens = B * S
        capacity = max(1, int(math.ceil(CAPACITY_FACTOR * tokens * k / E)))
        x2d = x.reshape(tokens, d)
        logits = x2d @ router_w.T + router_b
        vals, idx = jax.lax.top_k(logits, k)
        gates = jax.nn.softmax(vals, axis=-1)
        flat_e = idx.reshape(-1)
        oh = (flat_e[:, None] == jnp.arange(E)[None, :]).astype(jnp.int32)
        pos = jnp.take_along_axis(jnp.cumsum(oh, axis=0) - 1, flat_e[:, None], axis=1)[:, 0]
        kept = pos < capacity
        kept2 = kept.reshape(tokens, k)
        denom = jnp.sum(gates * kept2, axis=-1, keepdims=True)
        gates = jnp.where(kept2, gates / (denom + 1e-09), 0.0)
        slot = flat_e * capacity + pos
        slot_safe = jnp.where(kept, slot, E * capacity)
        x_rep = jnp.repeat(x2d, k, axis=0)
        buf = jnp.zeros((E * capacity + 1, d), x.dtype).at[slot_safe].set(x_rep)
        packed = buf[:E * capacity].reshape(E, capacity, d)
        h = jax.nn.gelu(jnp.einsum('ecd,edf->ecf', packed, w1) + b1[:, None, :], approximate=False)
        expert_out = jnp.einsum('ecf,efd->ecd', h, w2) + b2[:, None, :]
        eflat = expert_out.reshape(E * capacity, d)
        gathered = eflat[jnp.clip(slot, 0, E * capacity - 1)]
        w = (gates.reshape(-1) * kept.astype(x.dtype))[:, None]
        out = (gathered * w).reshape(tokens, k, d).sum(axis=1)
        return out.reshape(B, S, d)
    x = L0_attn_x
    x = x + 0.5 * _L0_ffn_ref(_layernorm(x, axis=-1), L0_ffn_router_w, L0_ffn_router_b, L0_ffn_w1, L0_ffn_b1, L0_ffn_w2, L0_ffn_b2)
    x = x + _L0_attn_ref(_layernorm(x, axis=-1), L0_attn_maa_x, L0_attn_maa_w, L0_attn_maa_k, L0_attn_maa_v, L0_attn_maa_r, L0_attn_maa_g, L0_attn_maa_w1, L0_attn_maa_w2, L0_attn_Wr, L0_attn_Wk, L0_attn_Wv, L0_attn_Wo, L0_attn_gate_w1, L0_attn_gate_w2, L0_attn_time_decay, L0_attn_decay_w1, L0_attn_decay_w2, L0_attn_u, L0_attn_ln_g, L0_attn_ln_b)
    x = x + 0.5 * _L0_ffn_ref(_layernorm(x, axis=-1), L0_ffn_router_w, L0_ffn_router_b, L0_ffn_w1, L0_ffn_b1, L0_ffn_w2, L0_ffn_b2)
    return x

_drawn_inputs = setup_inputs


def setup_inputs(seed=0):
    import zlib

    import numpy as np

    out = dict(_drawn_inputs(seed))
    spreads = {'L0_attn_ln_g': (1.0, 0.6),
     'L0_attn_ln_b': (0.0, 0.8),
     'L0_ffn_router_b': (0.0, 0.281),
     'L0_ffn_b1': (0.0, 0.296),
     'L0_ffn_b2': (0.0, 0.1)}
    factors = {'L0_attn_maa_x': 8.0,
     'L0_attn_maa_w': 200.0,
     'L0_attn_maa_k': 8.0,
     'L0_attn_maa_v': 8.0,
     'L0_attn_maa_r': 8.0,
     'L0_attn_maa_g': 8.0,
     'L0_attn_maa_w1': 8.0,
     'L0_attn_maa_w2': 8.0,
     'L0_attn_Wr': 3.97,
     'L0_attn_Wk': 3.971,
     'L0_attn_Wv': 3.966,
     'L0_attn_Wo': 3.96,
     'L0_attn_gate_w1': 3.972,
     'L0_attn_gate_w2': 3.993,
     'L0_attn_time_decay': 200.0,
     'L0_attn_decay_w1': 200.0,
     'L0_attn_decay_w2': 200.0,
     'L0_attn_u': 8.0}
    for name, (base, spread) in spreads.items():
        noise = np.random.default_rng([zlib.crc32(name.encode()), seed]).standard_normal(out[name].shape)
        drawn = base * np.exp(spread * noise) if base else spread * noise
        out[name] = jnp.asarray(drawn.astype(out[name].dtype))
    for name, factor in factors.items():
        out[name] = (out[name] * factor).astype(out[name].dtype)
    return out
```

```python
import concourse.bass as bass
from concourse import mybir
from contextlib import ExitStack

F32 = mybir.dt.float32
U32 = mybir.dt.uint32
ALU = mybir.AluOpType
ACT = mybir.ActivationFunctionType
AX = mybir.AxisListType

P = 128
T = 8192
SEQ = 1024
D = 256
DC = D // P
E = 16
TOPK = 2
CAP = 1280
DFF = 1024
FC = DFF // P
NT = T // P
GQ = 4
NG = NT // GQ
GT = GQ * P
BS = 256
NB = CAP // BS
H = 4
N = 64
LEVELS = 7
SKIP = 1 << 20


class Chain:

    def __init__(self, eng, sem, base=0):
        self.eng, self.sem, self.base, self.n = eng, sem, base, 0

    def __call__(self, ins):
        ins.then_inc(self.sem, 1)
        self.n += 1

    def settle(self):
        self.eng.wait_ge(self.sem, self.base + self.n)


def constants(nc, S):
    done, made, zeroed = S.sem("const_loaded"), S.sem("const_made"), S.sem("const_zeroed")
    filled = S.sem("slots_zeroed")
    with nc.Block() as block:
        @block.sync
        def _(sp):
            n = 0
            for dst, src in S.loads:
                sp.dma_start(dst, src).then_inc(done, 16)
                n += 16
            sp.wait_ge(zeroed, 1)
            rows = S.slots.rearrange("(a p b) d -> a p (b d)", p=P, b=10)
            for a in range(16):
                sp.dma_start(rows[a], S.zeros[:, :]).then_inc(filled, 16)
            sp.wait_ge(done, n)
            sp.wait_ge(filled, 16 * 16)

        @block.vector
        def _(dve):
            dve.memset(S.zeros[:, :], 0.0).then_inc(zeroed, 1)

        @block.gpsimd
        def _(pool):
            c = Chain(pool, made)
            c(pool.memset(S.ones[:, :], 1.0))
            c(pool.memset(S.eps[:, 0:1], 1e-5))
            c(pool.memset(S.eps[:, 1:2], 0.00064))
            c(pool.memset(S.ident[:, :], 0.0))
            c(pool.memset(S.before[:, :], 1.0))
            c(pool.memset(S.lev[:, :, :], 0))
            c(pool.iota(S.iota_i[:, :], pattern=[[1, E]], base=0, channel_multiplier=0))
            c.settle()
            c(pool.tensor_copy(S.iota_f[:, :], S.iota_i[:, :]))
            c(pool.affine_select(out=S.ident[:, :], in_=S.ident[:, :], compare_op=ALU.not_equal, fill=1.0,
                                 base=0, pattern=[[-1, P]], channel_multiplier=1))
            c(pool.affine_select(out=S.before[:, :], in_=S.before[:, :], compare_op=ALU.is_gt, fill=0.0,
                                 base=0, pattern=[[1, P]], channel_multiplier=-1))
            c.settle()


def level_masks(nc, S):
    made = S.sem("masks_made")
    with ExitStack() as ctx, nc.Block() as block:
        s_i = ctx.enter_context(nc.sbuf_tensor("mask_s", [P, N], mybir.dt.int32))
        t_i = ctx.enter_context(nc.sbuf_tensor("mask_t", [P, N], mybir.dt.int32))
        a_i = ctx.enter_context(nc.sbuf_tensor("mask_a", [P, 4, N], mybir.dt.int32))
        f_i = ctx.enter_context(nc.sbuf_tensor("mask_f", [P, 3, N], F32))
        iot = S.sem("mask_iota")

        @block.gpsimd
        def _(pool):
            pool.iota(s_i[:, :], pattern=[[0, N]], base=0, channel_multiplier=1).then_inc(iot, 1)
            pool.iota(t_i[:, :], pattern=[[1, N]], base=0, channel_multiplier=0).then_inc(iot, 1)

        @block.vector
        def _(dve):
            c = Chain(dve, made)
            dve.wait_ge(iot, 2)
            for l in range(6):
                c(dve.tensor_scalar(a_i[:, 0], s_i[:, :], l + 1, (N >> (l + 1)) - 1,
                                    ALU.logical_shift_right, ALU.bitwise_and))
                c(dve.tensor_scalar(a_i[:, 1], t_i[:, :], l + 1, None, ALU.logical_shift_right))
                c(dve.tensor_scalar(a_i[:, 2], s_i[:, :], l, 1, ALU.logical_shift_right, ALU.bitwise_and))
                c(dve.tensor_scalar(a_i[:, 3], t_i[:, :], l, 1, ALU.logical_shift_right, ALU.bitwise_and))
                c.settle()
                c(dve.tensor_tensor(f_i[:, 0], a_i[:, 0], a_i[:, 1], ALU.is_equal))
                c(dve.tensor_tensor(f_i[:, 1], a_i[:, 3], a_i[:, 2], ALU.is_gt))
                c.settle()
                c(dve.tensor_tensor(S.lev[:, l, :], f_i[:, 0], f_i[:, 1], ALU.mult))
                c.settle()
            c(dve.tensor_scalar(a_i[:, 0], s_i[:, :], N - 1, None, ALU.bitwise_and))
            c.settle()
            c(dve.tensor_tensor(S.diag[:, :], a_i[:, 0], t_i[:, :], ALU.is_equal))
            c.settle()


def layer_norm(dve, c, S, st, mv, rstd, rstd_at, x_tiles, out_tiles, ready):
    for q in range(GQ):
        c(dve.bn_stats(st[:, q, :], x_tiles(q)))
    c.settle()
    S.apart(dve)
    for q in range(GQ):
        c(dve.bn_aggr(mv[:, q, :], st[:, q, :]))
    c.settle()
    dve.sem_inc(S.var_ready, 1)
    dve.wait_ge(S.rstd_ready, rstd_at)
    c(dve.reciprocal(rstd, rstd))
    c.settle()
    for q in range(GQ):
        ins = dve.tensor_scalar(out_tiles(q), x_tiles(q), mv[:, q, 0:1], rstd[:, q:q + 1],
                                ALU.subtract, ALU.mult)
        if q < GQ - 1:
            c(ins)
    ins.then_inc(ready, 1)


def root(act, S, var, eps, out, at):
    act.wait_ge(S.var_ready, at)
    act.activation(out, var, ACT.Sqrt, bias=eps).then_inc(S.rstd_ready, 1)


def route(nc, S, tag):
    PER = 76
    with ExitStack() as ctx:
        def sb(name, shape, dt=F32):
            return ctx.enter_context(nc.sbuf_tensor(f"{tag}r_{name}", shape, dt))

        def ps(name, shape):
            return ctx.enter_context(nc.psum_tensor(f"{tag}r_{name}", shape, F32))

        def sem(name):
            return S.sem(f"{tag}_{name}")

        xn = [sb(f"xn{u}", [P, GQ, D]) for u in range(2)]
        xT = [sb(f"xT{u}", [P, DC, GT]) for u in range(2)]
        st = sb("st", [P, 2, GQ, 6])
        mv = sb("mv", [P, 2, GQ, 2])
        rstd = sb("rstd", [P, 2, GQ])
        logit = [sb(f"logit{u}", [P, GQ, E]) for u in range(2)]
        top = [sb(f"top{u}", [P, GQ, 8]) for u in range(2)]
        topi = [sb(f"topi{u}", [P, GQ, 8], U32) for u in range(2)]
        ef = [sb(f"ef{u}", [P, GQ, TOPK]) for u in range(2)]
        oh = [sb(f"oh{u}", [P, GQ * TOPK, E]) for u in range(2)]
        cnt = [sb(f"cnt{u}", [P, GQ, E]) for u in range(2)]
        sumc = sb("sumc", [P, E])
        seen = [sb(f"seen{u}", [P, E]) for u in range(2)]
        pex = [sb(f"pex{u}", [P, GQ * TOPK, E]) for u in range(2)]
        pos = [sb(f"pos{u}", [P, GQ, TOPK]) for u in range(2)]
        slot = [sb(f"slot{u}", [P, GQ, TOPK]) for u in range(2)]
        kept = [sb(f"kept{u}", [P, GQ, TOPK]) for u in range(2)]
        over = [sb(f"over{u}", [P, GQ, TOPK]) for u in range(2)]
        sidx = [sb(f"sidx{u}", [P, GQ, TOPK], U32) for u in range(2)]
        dif = [sb(f"dif{u}", [P, GQ]) for u in range(2)]
        ex = [sb(f"ex{u}", [P, GQ]) for u in range(2)]
        gt = [sb(f"gt{u}", [P, GQ, TOPK]) for u in range(2)]
        den = [sb(f"den{u}", [P, GQ]) for u in range(2)]
        pT = [ps(f"pT{c}", [P, GT]) for c in range(DC)]
        bank = [ps(f"bank{k}", [P, GT]) for k in range(4)]
        pL, pC = ([bank[k + u][:, 0:GQ * E].rearrange("p (q e) -> p q e", e=E) for u in range(2)] for k in (0, 2))

        x_loaded = [sem(f"x_loaded{u}") for u in range(2)]
        xn_ready = sem("xn_ready")
        transposed = sem("transposed")
        xT_ready = sem("xT_ready")
        logits_ready = sem("logits_ready")
        counts_ready = sem("counts_ready")
        seen_ready = sem("seen_ready")
        prefix_ready = sem("prefix_ready")
        dif_ready = sem("dif_ready")
        ex_ready = sem("ex_ready")
        sidx_ready = sem("sidx_ready")
        scattered = [sem(f"scattered{u}") for u in range(2)]
        chain = sem("route_chain")
        x_grp = S.x.rearrange("(g q p) d -> g p q d", p=P, q=GQ)

        with nc.Block() as block:
            if tag == "a":
                @block.sync
                def _(sp):
                    with sp.Fori(0, NG // 2) as i:
                        for u in range(2):
                            sp.wait_ge(x_loaded[u], i * 16)
                            sp.dma_start(S.x_sb[:, bass.ds((i * 2 + u) * GQ, GQ), :],
                                         x_grp[i * 2 + u]).then_inc(x_loaded[u], 16)

            @block.vector
            def _(dve):
                dve.memset(seen[0][:, :], 0.0).then_inc(seen_ready, 1)
                with dve.Fori(0, NG // 2) as i:
                    c = Chain(dve, chain, i * PER)
                    for u in range(2):
                        if tag == "a":
                            dve.wait_ge(x_loaded[u], i * 16 + 16)
                        dve.wait_ge(scattered[u], i * (16 * GQ * TOPK))
                        dve.wait_ge(transposed, i * 2)
                        layer_norm(dve, c, S, st[:, u], mv[:, u], rstd[:, u, :], i * 2 + (u + 1 + S.n_roots[tag]),
                                   lambda q: S.x_sb[:, (i * 2 + u) * GQ + q, :],
                                   lambda q: xn[u][:, q, :], xn_ready)
                    for u in range(2):
                        dve.wait_ge(logits_ready, i * 2 + u + 1)
                        c(dve.tensor_tensor(logit[u][:, :, :], pL[u][:, :, :],
                                            S.rb[:, :].unsqueeze(1).to_broadcast([P, GQ, E]), ALU.add))
                        c.settle()
                        S.apart(dve)
                        for q in range(GQ):
                            c(dve.max(top[u][:, q, :], logit[u][:, q, :]))
                        c.settle()
                        S.apart(dve)
                        for q in range(GQ):
                            c(dve.max_index(topi[u][:, q, :], top[u][:, q, :], logit[u][:, q, :]))
                        dve.wait_ge(ex_ready, i * 2 + u)
                        dve.tensor_tensor(dif[u][:, :], top[u][:, :, 1], top[u][:, :, 0],
                                          ALU.subtract).then_inc(dif_ready, 1)
                        c.settle()
                        c(dve.tensor_copy(ef[u][:, :, :], topi[u][:, :, 0:TOPK]))
                        c.settle()
                        c(dve.tensor_tensor(
                            oh[u][:, :, :],
                            S.iota_f[:, :].unsqueeze(1).to_broadcast([P, GQ * TOPK, E]),
                            ef[u][:, :, :].rearrange("p q k -> p (q k)").unsqueeze(2).to_broadcast([P, GQ * TOPK, E]),
                            ALU.is_equal))
                        c.settle()
                        ohk = oh[u][:, :, :].rearrange("p (q k) e -> p q k e", k=TOPK)
                        dve.wait_ge(prefix_ready, i * 2)
                        dve.tensor_tensor(cnt[u][:, :, :], ohk[:, :, 0, :], ohk[:, :, 1, :],
                                          ALU.add).then_inc(counts_ready, 1)
                        dve.wait_ge(counts_ready, i * 2 + u + 1)
                        c(dve.tensor_reduce(sumc[:, :], cnt[u][:, :, :].rearrange("p q e -> p e q"),
                                            AX.X, ALU.add))
                        c.settle()
                        if u == 1:
                            dve.wait_ge(prefix_ready, i * 2 + 1)
                        dve.wait_ge(seen_ready, i * 2 + u + 1)
                        dve.tensor_tensor(seen[1 - u][:, :], seen[u][:, :], sumc[:, :],
                                          ALU.add).then_inc(seen_ready, 1)
                    for u in range(2):
                        dve.wait_ge(prefix_ready, i * 2 + u + 1)
                        pexk = pex[u][:, :, :].rearrange("p (q k) e -> p q k e", k=TOPK)
                        ohk = oh[u][:, :, :].rearrange("p (q k) e -> p q k e", k=TOPK)
                        c(dve.tensor_tensor(pexk, ohk, pC[u][:, :, :].unsqueeze(2).to_broadcast([P, GQ, TOPK, E]),
                                            ALU.mult))
                        c.settle()
                        c(dve.tensor_reduce(pos[u][:, :, :].rearrange("p q k -> p (q k)"), pex[u][:, :, :],
                                            AX.X, ALU.add))
                        c.settle()
                        c(dve.tensor_scalar(kept[u][:, :, :], pos[u][:, :, :], float(CAP), None, ALU.is_lt))
                        c(dve.tensor_scalar(over[u][:, :, :], pos[u][:, :, :], float(CAP), float(SKIP),
                                            ALU.is_ge, ALU.mult))
                        c(dve.scalar_tensor_tensor(out=slot[u][:, :, :], in0=ef[u][:, :, :], scalar=float(CAP),
                                                   in1=pos[u][:, :, :], op0=ALU.mult, op1=ALU.add))
                        c.settle()
                        dve.tensor_tensor(sidx[u][:, :, :], slot[u][:, :, :], over[u][:, :, :],
                                          ALU.add).then_inc(sidx_ready, 1)
                        c(dve.tensor_scalar(S.gidx[:, bass.ds((i * 2 + u) * GQ, GQ), :], slot[u][:, :, :],
                                            float(E * CAP - 1), None, ALU.min))
                        dve.wait_ge(ex_ready, i * 2 + u + 1)
                        c(dve.tensor_scalar(den[u][:, :], ex[u][:, :], 1.0, None, ALU.add))
                        c.settle()
                        c(dve.reciprocal(gt[u][:, :, 0], den[u][:, :]))
                        c.settle()
                        c(dve.tensor_tensor(gt[u][:, :, 1], gt[u][:, :, 0], ex[u][:, :], ALU.mult))
                        c.settle()
                        c(dve.tensor_tensor(gt[u][:, :, :], gt[u][:, :, :], kept[u][:, :, :], ALU.mult))
                        c.settle()
                        c(dve.scalar_tensor_tensor(out=den[u][:, :], in0=gt[u][:, :, 0], scalar=1e-9,
                                                   in1=gt[u][:, :, 1], op0=ALU.add, op1=ALU.add))
                        c.settle()
                        c(dve.reciprocal(den[u][:, :], den[u][:, :]))
                        c.settle()
                        c(dve.tensor_scalar(den[u][:, :], den[u][:, :], 0.5, None, ALU.mult))
                        c.settle()
                        c(dve.tensor_tensor(S.gw[:, bass.ds((i * 2 + u) * GQ, GQ), :], gt[u][:, :, :],
                                            den[u][:, :].unsqueeze(2).to_broadcast([P, GQ, TOPK]), ALU.mult))
                    S.check(c.n, PER, tag + "route")

            @block.tensor
            def _(pe):
                with pe.Fori(0, NG // 2) as i:
                    for u in range(2):
                        pe.wait_ge(xn_ready, i * 2 + u + 1)
                        pe.wait_ge(xT_ready, i * 2 + u)
                        for q in range(GQ):
                            for k in range(DC):
                                t = pe.transpose(pT[k][:, q * P:(q + 1) * P], xn[u][:, q, k * P:(k + 1) * P],
                                                 S.ident[:, :])
                        t.then_inc(transposed, 1)
                    for u in range(2):
                        pe.wait_ge(xT_ready, i * 2 + u + 1)
                        for q in range(GQ):
                            for k in range(DC):
                                t = pe.matmul(pL[u][:, q, :], xT[u][:, k, q * P:(q + 1) * P], S.rwT[:, k, :],
                                              start=(k == 0), stop=(k == DC - 1))
                        t.then_inc(logits_ready, 1)
                    for u in range(2):
                        pe.wait_ge(counts_ready, i * 2 + u + 1)
                        pe.wait_ge(seen_ready, i * 2 + u + 1)
                        pe.matmul(pC[u][:, :, :], S.before[:, :], cnt[u][:, :, :], start=True, stop=False)
                        for j in range(GQ - 1):
                            pe.matmul(pC[u][:, j + 1:, :], S.ones[:, :],
                                      cnt[u][:, j:j + 1, :].to_broadcast([P, GQ - 1 - j, E]),
                                      start=False, stop=False)
                        pe.matmul(pC[u][:, :, :], S.ones[:, :],
                                  seen[u][:, :].unsqueeze(1).to_broadcast([P, GQ, E]),
                                  start=False, stop=True).then_inc(prefix_ready, 1)

            @block.scalar
            def _(act):
                with act.Fori(0, NG // 2) as i:
                    for u in range(2):
                        root(act, S, mv[:, u, :, 1], S.eps[:, 0:1], rstd[:, u], i * 2 + (u + 1 + S.n_roots[tag]))
                    for u in range(2):
                        act.wait_ge(transposed, i * 2 + u + 1)
                        act.wait_ge(logits_ready, i * 2)
                        act.copy(xT[u][:, 0, :], pT[0][:, :])
                        act.copy(xT[u][:, 1, :], pT[1][:, :]).then_inc(xT_ready, 1)
                    for u in range(2):
                        act.wait_ge(dif_ready, i * 2 + u + 1)
                        act.activation(ex[u][:, :], dif[u][:, :], ACT.Exp).then_inc(ex_ready, 1)

            @block.gpsimd
            def _(pool):
                with pool.Fori(0, NG // 2) as i:
                    for u in range(2):
                        pool.wait_ge(xn_ready, i * 2 + u + 1)
                        pool.wait_ge(sidx_ready, i * 2 + u + 1)
                        S.apart(pool)
                        for q in range(GQ):
                            for k in range(TOPK):
                                pool.indirect_dma_start(
                                    S.slots[:, :], bass.IndirectOffsetOnAxis(ap=sidx[u][:, q, k:k + 1], axis=0),
                                    xn[u][:, q, :], None, bounds_check=E * CAP - 1,
                                    oob_is_err=False).then_inc(scattered[u], 16)
                for u in range(2):
                    pool.wait_ge(scattered[u], NG // 2 * 16 * GQ * TOPK)


def experts(nc, S, tag):
    with ExitStack() as ctx:
        def sb(name, shape, dt=F32):
            return ctx.enter_context(nc.sbuf_tensor(f"{tag}e_{name}", shape, dt))

        def ps(name, shape):
            return ctx.enter_context(nc.psum_tensor(f"{tag}e_{name}", shape, F32))

        def sem(name):
            return S.sem(f"{tag}_{name}")

        w1 = [sb(f"w1_{u}", [P, DC, DFF]) for u in range(2)]
        w2 = [sb(f"w2_{u}", [P, FC, D]) for u in range(2)]
        xp = [sb(f"xp{b}", [P, 2, D]) for b in range(NB)]
        xT = [sb(f"xT{r}", [P, DC, BS]) for r in range(2)]
        hT = [sb(f"hT{r}", [P, FC, BS]) for r in range(2)]
        ob = [sb(f"ob{r}", [P, 2, D]) for r in range(2)]
        pT = [ps(f"pT{r}", [P, DC, BS]) for r in range(2)]
        HB = FC // 2
        pH = ps("pH", [P, FC, BS])
        pO = [ps(f"pO{r}", [P, 2, D]) for r in range(2)]

        w_loaded = [sem(f"w_loaded{u}") for u in range(2)]
        expert_done = [sem(f"expert_done{u}") for u in range(2)]
        xp_loaded = [sem(f"xp_loaded{b}") for b in range(NB)]
        xp_used = [sem(f"xp_used{b}") for b in range(NB)]
        xT_ready = [sem(f"exT_ready{r}") for r in range(2)]
        up_full = [sem(f"up_full{h}") for h in range(HB)]
        gelu_done = [sem(f"gelu_done{h}") for h in range(HB)]
        down_done = [sem(f"down_done{r}") for r in range(2)]
        out_ready = [sem(f"out_ready{r}") for r in range(2)]
        stored = [sem(f"stored{r}") for r in range(2)]

        w1_d = S.w1.rearrange("e (c p) f -> e p c f", p=P)
        w2_d = S.w2.rearrange("e (c p) d -> e p c d", p=P)
        xp_d = S.slots.rearrange("(n q p) d -> n p q d", p=P, q=2)
        eo_d = S.eout.rearrange("(n q p) d -> n p q d", p=P, q=2)
        M = 2 * NB

        def half(i, m):
            return i * (M // 2) + m // 2

        with nc.Block() as block:
            @block.sync
            def _(sp):
                def weights(u, e):
                    sp.dma_start(w1[u][:, :, :], w1_d[e]).then_inc(w_loaded[u], 16)
                    sp.dma_start(w2[u][:, :, :], w2_d[e]).then_inc(w_loaded[u], 16)

                with sp.Fori(0, E // 2) as i:
                    for u in range(2):
                        sp.wait_ge(expert_done[u], i)
                        weights(u, i * 2 + u)
                        for b in range(NB):
                            sp.wait_ge(xp_used[b], i * 2 + u)
                            sp.dma_start(xp[b][:, :, :], xp_d[i * M + (u * NB + b)]).then_inc(xp_loaded[b], 16)

            @block.tensor
            def _(pe):
                def turn(i, m):
                    b = m % NB
                    pe.wait_ge(xp_loaded[b], (i * 2 + m // NB) * 16 + 16)
                    pe.wait_ge(xT_ready[m % 2], half(i, m))
                    for q in range(2):
                        for k in range(DC):
                            t = pe.transpose(pT[m % 2][:, k, q * P:(q + 1) * P], xp[b][:, q, k * P:(k + 1) * P],
                                             S.ident[:, :])
                    t.then_inc(xp_used[b], 1)

                def up(i, m):
                    u = m // NB
                    pe.wait_ge(xT_ready[m % 2], half(i, m) + 1)
                    if m % NB == 0:
                        pe.wait_ge(w_loaded[u], i * 32 + 32)
                    for f in range(FC):
                        if f % 2 == 0:
                            pe.wait_ge(gelu_done[f // 2], i * M + m)
                        for k in range(DC):
                            t = pe.matmul(pH[:, f, :], w1[u][:, k, f * P:(f + 1) * P], xT[m % 2][:, k, :],
                                          start=(k == 0), stop=(k == DC - 1), skip_group_check=True)
                        if f % 2:
                            t.then_inc(up_full[f // 2], 1)

                def down(i, m):
                    u = m // NB
                    pe.wait_ge(out_ready[m % 2], half(i, m))
                    for h in range(HB):
                        pe.wait_ge(gelu_done[h], i * M + (m + 1))
                    for q in range(2):
                        for f in range(FC):
                            t = pe.matmul(pO[m % 2][:, q, :], hT[m % 2][:, f, q * P:(q + 1) * P], w2[u][:, f, :],
                                          start=(f == 0), stop=(f == FC - 1))
                    t.then_inc(down_done[m % 2], 1)
                    if m % NB == NB - 1:
                        pe.wait_ge(down_done[m % 2], half(i, m) + 1)
                        pe.sem_inc(expert_done[u], 1)

                with pe.Fori(0, E // 2) as i:
                    turn(i, 0)
                    for m in range(M):
                        up(i, m)
                        if m + 1 < M:
                            turn(i, m + 1)
                        if m:
                            down(i, m - 1)
                    down(i, M - 1)

            @block.scalar
            def _(act):
                with act.Fori(0, E // 2) as i:
                    def store(m):
                        act.wait_ge(out_ready[m % 2], half(i, m) + 1)
                        act.dma_start(eo_d[i * M + m], ob[m % 2][:, :, :]).then_inc(stored[m % 2], 16)

                    for m in range(M):
                        act.wait_ge(down_done[m % 2], half(i, m))
                        for f in range(FC):
                            if f % 2 == 0:
                                act.wait_ge(up_full[f // 2], i * M + (m + 1))
                                S.apart(act)
                            t = act.activation(hT[m % 2][:, f, :], pH[:, f, :], ACT.Gelu,
                                           bias=S.b1[:, bass.ds(i * (2 * FC) + ((m // NB) * FC + f), 1)])
                            if f % 2:
                                t.then_inc(gelu_done[f // 2], 1)
                        if m:
                            store(m - 1)
                    store(M - 1)
                for r in range(2):
                    act.wait_ge(stored[r], E // 2 * (M // 2) * 16)

            @block.vector
            def _(dve):
                with dve.Fori(0, E // 2) as i:
                    def turned(m):
                        dve.wait_ge(xp_used[m % NB], i * 2 + (m // NB + 1))
                        dve.wait_ge(up_full[HB - 1], i * M + max(m - 1, 0))
                        dve.tensor_copy(xT[m % 2][:, :, :], pT[m % 2][:, :, :]).then_inc(xT_ready[m % 2], 1)

                    def out(m):
                        dve.wait_ge(down_done[m % 2], half(i, m) + 1)
                        dve.wait_ge(stored[m % 2], half(i, m) * 16)
                        dve.tensor_tensor(ob[m % 2][:, :, :], pO[m % 2][:, :, :],
                                          S.b2[:, bass.ds(i * 2 + m // NB, 1), :].to_broadcast([P, 2, D]),
                                          ALU.add).then_inc(out_ready[m % 2], 1)

                    turned(0)
                    for m in range(M):
                        if m + 1 < M:
                            turned(m + 1)
                        if m:
                            out(m - 1)
                    out(M - 1)


def combine(nc, S, tag):
    last = tag == "b"
    with ExitStack() as ctx:
        rows = [ctx.enter_context(nc.sbuf_tensor(f"{tag}c_rows{u}", [P, GQ, TOPK, D], F32)) for u in range(2)]
        idx = [ctx.enter_context(nc.sbuf_tensor(f"{tag}c_idx{u}", [P, GQ, TOPK], U32)) for u in range(2)]
        idx_ready = S.sem(f"{tag}_idx_ready")
        gathered = [S.sem(f"{tag}_gathered{u}") for u in range(2)]
        first = S.sem(f"{tag}_first_added")
        added = S.sem(f"{tag}_added")
        out_stored = S.sem(f"{tag}_out_stored")
        o_grp = S.out.rearrange("(g q p) d -> g p q d", p=P, q=GQ)
        with nc.Block() as block:
            @block.vector
            def _(dve):
                with dve.Fori(0, NG // 2) as i:
                    for u in range(2):
                        dve.wait_ge(gathered[u], i * (16 * GQ * TOPK))
                        dve.tensor_copy(idx[u][:, :, :],
                                        S.gidx[:, bass.ds((i * 2 + u) * GQ, GQ), :]).then_inc(idx_ready, 1)
                    for u in range(2):
                        dve.wait_ge(gathered[u], i * (16 * GQ * TOPK) + 16 * GQ * TOPK)
                        for k in range(TOPK):
                            if k:
                                dve.wait_ge(first, i * (2 * GQ) + (u * GQ + GQ))
                            for q in range(GQ):
                                x = S.x_sb[:, (i * 2 + u) * GQ + q, :]
                                t = dve.scalar_tensor_tensor(
                                    out=x, in0=rows[u][:, q, k, :], scalar=S.gw[:, (i * 2 + u) * GQ + q, k:k + 1],
                                    in1=x, op0=ALU.mult, op1=ALU.add)
                                t.then_inc(first if k == 0 else added, 1)

            @block.gpsimd
            def _(pool):
                with pool.Fori(0, NG // 2) as i:
                    for u in range(2):
                        pool.wait_ge(idx_ready, i * 2 + u + 1)
                        pool.wait_ge(added, i * (2 * GQ))
                        S.apart(pool)
                        for q in range(GQ):
                            for k in range(TOPK):
                                pool.indirect_dma_start(
                                    rows[u][:, q, k, :], None, S.eout[:, :],
                                    bass.IndirectOffsetOnAxis(ap=idx[u][:, q, k:k + 1], axis=0)
                                ).then_inc(gathered[u], 16)

            if last:
                @block.sync
                def _(sp):
                    with sp.Fori(0, NG) as g:
                        sp.wait_ge(added, g * GQ + GQ)
                        sp.dma_start(o_grp[g], S.x_sb[:, bass.ds(g * GQ, GQ), :]).then_inc(out_stored, 16)
                    sp.wait_ge(out_stored, NG * 16)


def mix(nc, S):
    G2 = SEQ // GT
    NJ = 36
    NBK = 4
    DPER = None
    with ExitStack() as ctx:
        def sb(name, shape, dt=F32):
            return ctx.enter_context(nc.sbuf_tensor(f"m_{name}", shape, dt))

        def sem(name):
            return S.sem(f"m_{name}")

        xn = sb("xn", [P, GQ, D])
        st = sb("st", [P, GQ, 6])
        mv = sb("mv", [P, GQ, 2])
        rstd = sb("rstd", [P, GQ])
        xT = sb("xT", [P, DC, GT + 1])
        xx = sb("xx", [P, DC, GT])
        xxx = sb("xxx", [P, DC, GT])
        lora = sb("lora", [P, GT])
        lorag = sb("lorag", [32, GT])
        tmp = [sb(f"tmp{j}", [P, GT]) for j in range(2)]
        xf = [sb(f"xf{f}", [P, DC, GT]) for f in range(5)]
        tw = sb("tw", [N, GT])
        tg = sb("tg", [N, GT])
        W = sb("W", [P, DC * GT])
        tot = [W] + [sb(f"tot{l}", [P, DC * GT >> l]) for l in range(1, LEVELS + 1)]
        RP = sb("RP", [P, DC, GT])
        KS = sb("KS", [P, DC, GT])
        RU = sb("RU", [P, DC, GT])
        V = sb("V", [P, GQ, D])
        G = sb("G", [P, GQ, D])
        A = sb("A", [P, 2 * GQ * 2, N])
        Af = sb("Af", [P, 2 * GQ * 2, P])
        KR = sb("KR", [P, GQ, D])
        Sbd = sb("Sbd", [P, 2, P])
        Y = sb("Y", [P, GQ, D])
        Y2 = sb("Y2", [P, GQ, D])
        mean = sb("mean", [P, GQ * H])
        var = sb("var", [P, GQ * H])
        rvar = sb("rvar", [P, GQ * H])
        ygT = sb("ygT", [P, DC, GT])
        B = [ctx.enter_context(nc.psum_tensor(f"m_B{k}", [P, GT], F32)) for k in range(NBK)]
        PX = ctx.enter_context(nc.psum_tensor("m_PX", [P, 2, GT], F32))
        PA = ctx.enter_context(nc.psum_tensor("m_PA", [P, 2, GT], F32))

        filled = [sem(f"filled{k}") for k in range(NBK)]
        drained = [sem(f"drained{k}") for k in range(NBK)]
        xn_ready = sem("xn_ready")
        carry_ready = sem("carry_ready")
        turned = sem("turned")
        xT_ready = sem("xT_ready")
        xxx_ready = sem("xxx_ready")
        tanh_ready = sem("tanh_ready")
        mixed = [sem(f"mixed{j}") for j in range(2)]
        tmp_ready = [sem(f"tmp_ready{j}") for j in range(2)]
        kr_ready = sem("kr_ready")
        wl_ready = sem("wl_ready")
        w_ready = sem("w_ready")
        ru_ready = sem("ru_ready")
        v_ready = sem("v_ready")
        g_ready = sem("g_ready")
        prod_ready = sem("prod_ready")
        prod_used = sem("prod_used")
        level_ready = sem("level_ready")
        ks_turned = sem("ks_turned")
        af_ready = sem("af_ready")
        a_zero = sem("a_zero")
        krow_ready = sem("krow_ready")
        state_ready = sem("state_ready")
        y_ready = sem("y_ready")
        yc_ready = sem("yc_ready")
        sq_ready = sem("sq_ready")
        yn_ready = sem("yn_ready")
        yg_ready = sem("yg_ready")
        yg_turned = sem("yg_turned")
        ygT_ready = sem("ygT_ready")
        dchain = sem("mix_vector_chain")
        achain = sem("mix_scalar_chain")
        pchain = sem("mix_pool_chain")

        JB = NJ // NBK

        def fill(pe, g, j):
            pe.wait_ge(drained[j % NBK], g * JB + j // NBK)
            return B[j % NBK]

        def full(eng, g, j):
            eng.wait_ge(filled[j % NBK], g * JB + (j // NBK + 1))
            return B[j % NBK]

        LORA, LORAG, M0, DW1, GW1, K0, R0, DW2, V0, G0, ST0, Y0, O0 = 0, 1, 2, 12, 13, 14, 16, 18, 20, 22, 24, 25, 32
        VCH, SCH, PCH = 67, 1, 1

        def blocks(a, l):
            return a.rearrange("p (b h s) -> p b h s", h=2, s=1 << l)

        with nc.Block() as block:
            @block.vector
            def _(dve):
                with dve.Fori(0, T // SEQ) as i:
                    c = Chain(dve, dchain, i * (2 * S.VPER))
                    for u in range(2):
                        g = i * 2 + u
                        if u == 0:
                            dve.memset(xT[:, :, 0:1], 0.0).then_inc(carry_ready, 1)
                            c(dve.memset(Sbd[:, :, :], 0.0))
                        else:
                            dve.tensor_copy(xT[:, :, 0:1], xT[:, :, GT:GT + 1]).then_inc(carry_ready, 1)
                            c(dve.memset(mean[:, :], 0.0))
                        layer_norm(dve, c, S, st, mv, rstd[:, :], i * 4 + (2 * u + 1 + S.n_roots["mix"]), lambda q: S.x_sb[:, g * GQ + q, :],
                                   lambda q: xn[:, q, :], xn_ready)
                        dve.wait_ge(xT_ready, g + 1)
                        c(dve.tensor_tensor(xx[:, :, :], xT[:, :, 0:GT], xT[:, :, 1:GT + 1], ALU.subtract))
                        c.settle()
                        for k in range(DC):
                            t = dve.scalar_tensor_tensor(out=xxx[:, k, :], in0=xx[:, k, :], scalar=S.ch[:, 0, k:k + 1],
                                                         in1=xT[:, k, 1:GT + 1], op0=ALU.mult, op1=ALU.add)
                            t.then_inc(xxx_ready, 1)
                        for j in range(10):
                            f, k = j // 2, j % 2
                            b = full(dve, g, M0 + j)
                            dve.wait_ge(mixed[k], g * 5 + f)
                            c(dve.scalar_tensor_tensor(out=tmp[k][:, :], in0=b[:, :], scalar=S.ch[:, 1 + f, k:k + 1],
                                                       in1=xx[:, k, :], op0=ALU.add, op1=ALU.mult))
                            c.settle()
                            dve.sem_inc(drained[(M0 + j) % NBK], 1)
                            dve.sem_inc(tmp_ready[k], 1)
                        for k in range(DC):
                            b = full(dve, g, DW2 + k)
                            c(dve.tensor_scalar(tot[1][:, :] if k == 0 else xxx[:, 0, :], b[:, :],
                                                S.ch[:, 6, k:k + 1], 10.0, ALU.add, ALU.min))
                            c.settle()
                            dve.sem_inc(drained[(DW2 + k) % NBK], 1)
                            dve.sem_inc(wl_ready, 1)
                        dve.wait_ge(kr_ready, g * 4 + 4)
                        for k in range(DC):
                            dve.tensor_scalar(RU[:, k, :], RP[:, k, :], S.ch[:, 7, k:k + 1], None,
                                              ALU.mult).then_inc(ru_ready, 1)
                        dve.wait_ge(prod_ready, g * 8 + 1)
                        pa = lambda t: t[:, :, :].rearrange("p h (r n) -> p (h r) n", n=N)
                        c(dve.tensor_tensor(A[:, :, :], pa(PA),
                                            S.diag[:, :].unsqueeze(1).to_broadcast([P, 16, N]), ALU.mult))
                        c.settle()
                        dve.sem_inc(prod_used, 1)
                        dve.wait_ge(w_ready, g * 2 + 2)
                        flat = lambda t: t[:, :, :].rearrange("p c t -> p (c t)")
                        for l in range(LEVELS):
                            dve.wait_ge(prod_ready, g * 8 + (l + 2))
                            rp, ks = blocks(flat(RP), l), blocks(flat(KS), l)
                            tl = tot[l][:, :].rearrange("p (b h) -> p b h", h=2)
                            nb = DC * GT >> (l + 1)
                            shape = [P, nb, 1 << l]
                            c(dve.tensor_tensor(rp[:, :, 1, :], rp[:, :, 1, :], tl[:, :, 0:1].to_broadcast(shape), ALU.mult))
                            c(dve.tensor_tensor(ks[:, :, 0, :], ks[:, :, 0, :], tl[:, :, 1:2].to_broadcast(shape), ALU.mult))
                            c(dve.tensor_tensor(tot[l + 1][:, :], tl[:, :, 0], tl[:, :, 1], ALU.mult))
                            c.settle()
                            dve.sem_inc(level_ready, 1)
                            if l < 6:
                                c(dve.copy_predicated(A[:, :, :], S.lev[:, l, :].unsqueeze(1).to_broadcast([P, 16, N]),
                                                      pa(PX if l % 2 == 0 else PA)))
                                c.settle()
                                dve.sem_inc(prod_used, 1)
                        for q in range(GQ):
                            b = full(dve, g, ST0 + 2 * q)
                            full(dve, g, Y0 + 2 * q)
                            bs = b[:, 0:2 * P].rearrange("p (r n) -> p r n", n=P)
                            for r in range(2):
                                for h in range(2):
                                    rows = slice(h * N, h * N + N)
                                    t = dve.scalar_tensor_tensor(
                                        out=Sbd[rows, r, rows], in0=Sbd[rows, r, rows],
                                        scalar=tot[LEVELS][rows, r * GQ + q:r * GQ + q + 1],
                                        in1=bs[rows, r, rows], op0=ALU.mult, op1=ALU.add)
                                    c(t)
                            c.settle()
                            dve.sem_inc(state_ready, 1)
                            dve.sem_inc(drained[(ST0 + 2 * q) % NBK], 1)
                        dve.wait_ge(y_ready, g * GQ + GQ)
                        yh = lambda t: t[:, :, :].rearrange("p q (h n) -> p (q h) n", n=N)
                        bc = lambda t: t[:, :].unsqueeze(2).to_broadcast([P, GQ * H, N])
                        c(dve.tensor_reduce(mean[:, :], yh(Y), AX.X, ALU.add))
                        c.settle()
                        c(dve.tensor_scalar(mean[:, :], mean[:, :], 1.0 / N, None, ALU.mult))
                        c.settle()
                        dve.tensor_tensor(yh(Y), yh(Y), bc(mean), ALU.subtract).then_inc(yc_ready, 1)
                        dve.wait_ge(sq_ready, g + 1)
                        c(dve.tensor_reduce(var[:, :], yh(Y2), AX.X, ALU.add))
                        c.settle()
                        dve.tensor_scalar(var[:, :], var[:, :], 1.0 / N, None, ALU.mult).then_inc(S.var_ready, 1)
                        dve.wait_ge(S.rstd_ready, i * 4 + (2 * u + 2 + S.n_roots["mix"]))
                        c(dve.reciprocal(rvar[:, :], rvar[:, :]))
                        c.settle()
                        dve.wait_ge(yc_ready, g + 1)
                        c(dve.tensor_tensor(yh(Y), yh(Y), bc(rvar), ALU.mult))
                        c.settle()
                        dve.tensor_tensor(Y[:, :, :], Y[:, :, :], S.ln_g[:, :].unsqueeze(1).to_broadcast([P, GQ, D]),
                                          ALU.mult).then_inc(yn_ready, 1)
                        for q in range(GQ):
                            b = full(dve, g, O0 + q)
                            x = S.x_sb[:, g * GQ + q, :]
                            dve.tensor_tensor(x, x, b[:, 0:D], ALU.add).then_inc(drained[(O0 + q) % NBK], 1)
                    S.check(c.n, 2 * S.VPER, "mix vector")

            @block.gpsimd
            def _(pool):
                pool.memset(Af[:, :, :], 0.0).then_inc(a_zero, 1)
                with pool.Fori(0, T // SEQ) as i:
                    for u in range(2):
                        g = i * 2 + u
                        for j in range(10):
                            f, k = j // 2, j % 2
                            pool.wait_ge(tmp_ready[k], g * 5 + (f + 1))
                            pool.tensor_tensor(xf[f][:, k, :], tmp[k][:, :], xT[:, k, 1:GT + 1],
                                               ALU.add).then_inc(mixed[k], 1)
                        pool.wait_ge(yn_ready, g + 1)
                        pool.tensor_tensor(Y[:, :, :], Y[:, :, :], S.ln_b[:, :].unsqueeze(1).to_broadcast([P, GQ, D]),
                                           ALU.add).then_inc(pchain, 1)
                        pool.wait_ge(pchain, g + 1)
                        pool.wait_ge(g_ready, g * 2 + 2)
                        pool.tensor_tensor(Y2[:, :, :], Y[:, :, :], G[:, :, :], ALU.mult).then_inc(yg_ready, 1)

            @block.scalar
            def _(act):
                with act.Fori(0, T // SEQ) as i:
                    for u in range(2):
                        g = i * 2 + u
                        root(act, S, mv[:, :, 1], S.eps[:, 0:1], rstd[:, :], i * 4 + (2 * u + 1 + S.n_roots["mix"]))
                        act.wait_ge(turned, g + 1)
                        act.wait_ge(carry_ready, g + 1)
                        act.copy(xT[:, :, 1:GT + 1], PX[:, :, :]).then_inc(xT_ready, 1)

                        def drain(j, out, in_, func, ready):
                            act.activation(out, in_, func).then_inc(ready, 1)

                        b = full(act, g, LORA)
                        act.activation(lora[:, :], b[:, :], ACT.Tanh).then_inc(drained[LORA % NBK], 1)
                        b = full(act, g, LORAG)
                        act.activation(lorag[:, :], b[0:32, :], ACT.Tanh).then_inc(drained[LORAG % NBK], 1)
                        b = full(act, g, DW1)
                        act.activation(tw[:, :], b[0:N, :], ACT.Tanh).then_inc(drained[DW1 % NBK], 1)
                        b = full(act, g, GW1)
                        act.activation(tg[:, :], b[0:N, :], ACT.Tanh).then_inc(drained[GW1 % NBK], 1)
                        for j, t in ((K0, KS), (R0, RP)):
                            for k in range(DC):
                                b = full(act, g, j + k)
                                act.copy(t[:, k, :], b[:, :]).then_inc(drained[(j + k) % NBK], 1)
                                act.wait_ge(drained[(j + k) % NBK], g * JB + ((j + k) // NBK + 1))
                                act.sem_inc(kr_ready, 1)
                        for k in range(DC):
                            act.wait_ge(wl_ready, g * 2 + k + 1)
                            src = tot[1][:, :] if k == 0 else xxx[:, 0, :]
                            act.activation(xxx[:, 1, :] if k else Y2[:, 0:2, :].rearrange("p a b -> p (a b)"), src,
                                           ACT.Exp).then_inc(achain, 1)
                        act.wait_ge(achain, g * 2 + 2)
                        for k in range(DC):
                            act.activation(W[:, k * GT:(k + 1) * GT],
                                           xxx[:, 1, :] if k else Y2[:, 0:2, :].rearrange("p a b -> p (a b)"),
                                           ACT.Exp, scale=-1.0).then_inc(w_ready, 1)
                        for j, t in ((V0, V), (G0, G)):
                            for k in range(2):
                                b = full(act, g, j + k)
                                act.copy(t[:, 2 * k:2 * k + 2, :],
                                         b[:, :].rearrange("p (q d) -> p q d", d=D)).then_inc(drained[(j + k) % NBK], 1)
                                act.wait_ge(drained[(j + k) % NBK], g * JB + ((j + k) // NBK + 1))
                                act.sem_inc(v_ready if t is V else g_ready, 1)
                        act.wait_ge(a_zero, 1)
                        act.wait_ge(prod_ready, g * 8 + 8)
                        act.copy(Af[0:N, :, N:P], PX[0:N, :, :].rearrange("p h (r n) -> p (h r) n", n=N)
                                 ).then_inc(af_ready, 1)
                        act.wait_ge(prod_used, g * 7 + 7)
                        act.copy(Af[0:N, :, 0:N], A[0:N, :, :]).then_inc(af_ready, 1)
                        act.copy(Af[N:P, :, N:P], A[N:P, :, :]).then_inc(af_ready, 1)
                        act.wait_ge(ks_turned, g + 1)
                        act.copy(KR[:, :, :].rearrange("p (a q) d -> p a (q d)", a=2), PA[:, :, :]
                                 ).then_inc(krow_ready, 1)
                        for q in range(GQ):
                            b = full(act, g, Y0 + 2 * q)
                            act.copy(Y[:, q, :], b[:, 0:D]).then_inc(drained[(Y0 + 2 * q) % NBK], 1)
                            act.wait_ge(drained[(Y0 + 2 * q) % NBK], g * JB + ((Y0 + 2 * q) // NBK + 1))
                            act.sem_inc(y_ready, 1)
                        act.wait_ge(yc_ready, g + 1)
                        act.activation(Y2[:, :, :], Y[:, :, :], ACT.Square).then_inc(sq_ready, 1)
                        root(act, S, var[:, :], S.eps[:, 1:2], rvar[:, :], i * 4 + (2 * u + 2 + S.n_roots["mix"]))
                        act.wait_ge(yg_turned, g + 1)
                        act.copy(ygT[:, :, :], PX[:, :, :]).then_inc(ygT_ready, 1)

            @block.tensor
            def _(pe):
                pairs = [(r, h) for r in range(2) for h in range(2)]

                def halves(dst, ks, rp):
                    for q in range(GQ):
                        for c in range(2):
                            ts = slice(q * P + c * N, q * P + c * N + N)
                            for r, h in pairs:
                                rows = slice(h * N, h * N + N)
                                t = pe.matmul(dst[c * N:c * N + N, h, (q * 2 + r) * N:(q * 2 + r + 1) * N],
                                              ks[rows, r, ts], rp[rows, r, ts], start=True, stop=True,
                                              skip_group_check=True)
                    t.then_inc(prod_ready, 1)

                with pe.Fori(0, T // SEQ) as i:
                    for u in range(2):
                        g = i * 2 + u
                        pe.wait_ge(xn_ready, g + 1)
                        pe.wait_ge(ygT_ready, g)
                        for q in range(GQ):
                            for k in range(DC):
                                t = pe.transpose(PX[:, k, q * P:(q + 1) * P], xn[:, q, k * P:(k + 1) * P], S.ident[:, :])
                        t.then_inc(turned, 1)
                        pe.wait_ge(xxx_ready, g * 2 + 2)
                        b = fill(pe, g, LORA)
                        for k in range(DC):
                            t = pe.matmul(b[:, :], S.maa_w1[:, k, 0:P], xxx[:, k, :], start=(k == 0), stop=(k == 1))
                        t.then_inc(filled[LORA % NBK], 1)
                        b = fill(pe, g, LORAG)
                        for k in range(DC):
                            t = pe.matmul(b[0:32, :], S.maa_w1[:, k, P:160], xxx[:, k, :], start=(k == 0), stop=(k == 1))
                        t.then_inc(filled[LORAG % NBK], 1)
                        pe.wait_ge(drained[LORA % NBK], g * JB + 1)
                        pe.wait_ge(drained[LORAG % NBK], g * JB + 1)
                        for j in range(10):
                            f, k = j // 2, j % 2
                            b = fill(pe, g, M0 + j)
                            if f < 4:
                                t = pe.matmul(b[:, :], S.maa_w2[32 * f:32 * f + 32, k * P:(k + 1) * P],
                                              lora[32 * f:32 * f + 32, :], start=True, stop=True,
                                              tile_position=(32 * f, 0))
                            else:
                                t = pe.matmul(b[:, :], S.maa_w2g[:, k * P:(k + 1) * P], lorag[:, :],
                                              start=True, stop=True)
                            t.then_inc(filled[(M0 + j) % NBK], 1)

                        def mixed_in(f):
                            for k in range(DC):
                                pe.wait_ge(mixed[k], g * 5 + (f + 1))

                        def project(j, w, x, n=P, o=0):
                            b = fill(pe, g, j)
                            for k in range(DC):
                                t = pe.matmul(b[0:n, :], w[:, k, o:o + n], x[:, k, :], start=(k == 0), stop=(k == 1))
                            t.then_inc(filled[j % NBK], 1)

                        mixed_in(0)
                        project(DW1, S.dw1, xf[0], N)
                        mixed_in(4)
                        project(GW1, S.gw1, xf[4], N)
                        for k in range(DC):
                            project(K0 + k, S.Wk, xf[1], P, k * P)
                        for k in range(DC):
                            project(R0 + k, S.Wr, xf[3], P, k * P)
                        pe.wait_ge(drained[DW1 % NBK], g * JB + (DW1 // NBK + 1))
                        for k in range(DC):
                            b = fill(pe, g, DW2 + k)
                            pe.matmul(b[:, :], S.dw2[:, k * P:(k + 1) * P], tw[:, :], start=True,
                                      stop=True).then_inc(filled[(DW2 + k) % NBK], 1)
                        for a in range(2):
                            b = fill(pe, g, V0 + a)
                            for q in range(2):
                                for k in range(DC):
                                    s = (2 * a + q) * P
                                    t = pe.matmul(b[:, q * D:(q + 1) * D], xf[2][:, k, s:s + P], S.Wv[:, k, :],
                                                  start=(k == 0), stop=(k == 1))
                            t.then_inc(filled[(V0 + a) % NBK], 1)
                        pe.wait_ge(drained[GW1 % NBK], g * JB + (GW1 // NBK + 1))
                        for a in range(2):
                            b = fill(pe, g, G0 + a)
                            for q in range(2):
                                s = (2 * a + q) * P
                                t = pe.matmul(b[:, q * D:(q + 1) * D], tg[:, s:s + P], S.gw2[:, :], start=True, stop=True)
                            t.then_inc(filled[(G0 + a) % NBK], 1)
                        pe.wait_ge(ru_ready, g * 2 + 2)
                        pe.wait_ge(kr_ready, g * 4 + 4)
                        S.apart(pe)
                        halves(PA, KS, RU)
                        halves(PX, KS, RP)
                        for l in range(1, 6):
                            pe.wait_ge(level_ready, g * 7 + l)
                            pe.wait_ge(prod_used, g * 7 + l)
                            S.apart(pe)
                            halves(PX if l % 2 == 0 else PA, KS, RP)
                        pe.wait_ge(level_ready, g * 7 + 6)
                        pe.wait_ge(prod_used, g * 7 + 6)
                        S.apart(pe)
                        for q in range(GQ):
                            for r, h in pairs:
                                rows = slice(h * N, h * N + N)
                                t = pe.matmul(PX[0:N, h, (q * 2 + r) * N:(q * 2 + r + 1) * N],
                                              KS[rows, r, q * P:q * P + N], RP[rows, r, q * P + N:(q + 1) * P],
                                              start=True, stop=True, skip_group_check=True)
                        t.then_inc(prod_ready, 1)
                        pe.wait_ge(level_ready, g * 7 + 7)
                        pe.wait_ge(prod_used, g * 7 + 7)
                        for q in range(GQ):
                            for r in range(2):
                                t = pe.transpose(PA[:, q // 2, (q % 2) * D + r * P:(q % 2) * D + (r + 1) * P],
                                                 KS[:, r, q * P:(q + 1) * P], S.ident[:, :])
                        t.then_inc(ks_turned, 1)
                        pe.wait_ge(krow_ready, g + 1)
                        pe.wait_ge(v_ready, g * 2 + 2)
                        pe.wait_ge(af_ready, g * 3 + 3)
                        for q in range(GQ):
                            b = fill(pe, g, ST0 + 2 * q)
                            for r in range(2):
                                rs = slice(r * P, (r + 1) * P)
                                t = pe.matmul(b[:, rs], KR[:, q, rs], V[:, q, rs], start=True, stop=True)
                            t.then_inc(filled[(ST0 + 2 * q) % NBK], 1)
                            b = fill(pe, g, Y0 + 2 * q)
                            pe.wait_ge(state_ready, g * GQ + q)
                            for r in range(2):
                                rs = slice(r * P, (r + 1) * P)
                                pe.matmul(b[:, rs], RP[:, r, q * P:(q + 1) * P], Sbd[:, r, :], start=(r == 0), stop=False,
                                          skip_group_check=True)
                            for r, h in pairs:
                                cs = slice(r * P + h * N, r * P + h * N + N)
                                t = pe.matmul(b[:, cs], Af[:, (h * GQ + q) * 2 + r, :], V[:, q, cs], start=False,
                                              stop=(r == 1 and h == 1), skip_group_check=True)
                            t.then_inc(filled[(Y0 + 2 * q) % NBK], 1)
                        pe.wait_ge(yg_ready, g + 1)
                        for q in range(GQ):
                            for k in range(DC):
                                t = pe.transpose(PX[:, k, q * P:(q + 1) * P], Y2[:, q, k * P:(k + 1) * P], S.ident[:, :])
                        t.then_inc(yg_turned, 1)
                        pe.wait_ge(ygT_ready, g + 1)
                        for q in range(GQ):
                            b = fill(pe, g, O0 + q)
                            for k in range(DC):
                                t = pe.matmul(b[:, 0:D], ygT[:, k, q * P:(q + 1) * P], S.Wo[:, k, :],
                                              start=(k == 0), stop=(k == 1))
                            t.then_inc(filled[(O0 + q) % NBK], 1)


class Shared:

    def __init__(self, nc, ctx):
        self.nc, self.ctx = nc, ctx

    def sem(self, name):
        return self.ctx.enter_context(self.nc.semaphore(name))

    def apart(self, eng):
        eng.sem_inc(self.passed, 1)

    def check(self, n, want, what):
        assert n == want, (what, n, want)


def store_x(nc, S):
    s = S.sem("dbg")
    with nc.Block() as block:
        @block.sync
        def _(sp):
            sp.dma_start(S.out.rearrange("(g p) d -> p g d", p=P), S.x_sb[:, :, :]).then_inc(s, 16)
            sp.wait_ge(s, 16)


DEBUG = None
VPER = 75


def program(nc, x, rwT, rb, w1, b1T, w2, b2, chvec, maa_w1, maa_w2, Wr, Wk, Wv, Wo, gw1, gw2, dw1, dw2,
            ln_g, ln_b, out, debug=None):
    with ExitStack() as ctx:
        S = Shared(nc, ctx)

        def sb(name, shape, dt=F32):
            return ctx.enter_context(nc.sbuf_tensor(name, shape, dt))

        S.VPER = VPER
        S.var_ready = S.sem("var_ready")
        S.rstd_ready = S.sem("rstd_ready")
        S.passed = S.sem("passed")
        S.n_roots = {"a": 0, "mix": NG, "b": 3 * NG}
        S.x, S.w1, S.w2, S.out = x, w1, w2, out
        S.slots = nc.dram_tensor("slots", [E * CAP, D], F32, kind="Internal").ap()
        S.eout = nc.dram_tensor("eout", [E * CAP, D], F32, kind="Internal").ap()
        S.x_sb = sb("x_sb", [P, NT, D])
        S.gidx = sb("gidx", [P, NT, TOPK], U32)
        S.gw = sb("gw", [P, NT, TOPK])
        S.b1 = sb("b1", [P, E * FC])
        S.b2 = sb("b2", [P, E, D])
        S.rb = sb("rb", [P, E])
        S.rwT = sb("rwT", [P, DC, E])
        S.eps = sb("eps", [P, 2])
        S.ident = sb("ident", [P, P])
        S.before = sb("before", [P, P])
        S.ones = sb("ones", [P, P])
        S.iota_i = sb("iota_i", [P, E], mybir.dt.int32)
        S.iota_f = sb("iota_f", [P, E])
        S.lev = sb("lev", [P, 6, N], mybir.dt.int32)
        S.diag = sb("diag", [P, N])
        S.ch = sb("ch", [P, 8, DC])
        S.maa_w1 = sb("maa_w1", [P, DC, 160])
        S.maa_w2 = sb("maa_w2", [P, D])
        S.maa_w2g = sb("maa_w2g", [32, D])
        S.Wr, S.Wk, S.Wv, S.Wo = (sb(n, [P, DC, D]) for n in ("Wr", "Wk", "Wv", "Wo"))
        S.gw1 = sb("gw1", [P, DC, N])
        S.gw2 = sb("gw2", [N, D])
        S.dw1 = sb("dw1", [P, DC, N])
        S.dw2 = sb("dw2", [N, D])
        S.ln_g = sb("ln_g", [P, D])
        S.ln_b = sb("ln_b", [P, D])
        rows = lambda w: w.rearrange("(c p) n -> p c n", p=P)
        S.loads = [
            (S.b1[:, :], b1T), (S.b2[:, :, :].rearrange("p e d -> p (e d)"), b2.partition_broadcast(P)),
            (S.rb[:, :], rb.partition_broadcast(P)), (S.rwT[:, :, :], rows(rwT)), (S.ch[:, :, :], chvec),
            (S.maa_w1[:, :, :], rows(maa_w1)), (S.maa_w2[:, :], maa_w2[0:P, :]), (S.maa_w2g[:, :], maa_w2[P:160, :]),
            (S.Wr[:, :, :], rows(Wr)), (S.Wk[:, :, :], rows(Wk)), (S.Wv[:, :, :], rows(Wv)), (S.Wo[:, :, :], rows(Wo)),
            (S.gw1[:, :, :], rows(gw1)), (S.gw2[:, :], gw2), (S.dw1[:, :, :], rows(dw1)), (S.dw2[:, :], dw2),
            (S.ln_g[:, :], ln_g.partition_broadcast(P)), (S.ln_b[:, :], ln_b.partition_broadcast(P)),
        ]
        with nc.sbuf_tensor("zeros", [P, 2560], F32) as zeros:
            S.zeros = zeros
            constants(nc, S)
        level_masks(nc, S)
        route(nc, S, "a")
        experts(nc, S, "a")
        if debug == "ffn":
            combine(nc, S, "b")
            return
        combine(nc, S, "a")
        mix(nc, S)
        if debug == "mix":
            store_x(nc, S)
            return
        route(nc, S, "b")
        experts(nc, S, "b")
        combine(nc, S, "b")

def kernel(**inputs):
    import numpy as np
    import concourse.bacc as bacc
    from concourse.bass_utils import run_bass_kernel_spmd

    f = lambda k: np.asarray(inputs[k])
    att = lambda k: f("L0_attn_" + k)
    ffn = lambda k: f("L0_ffn_" + k)
    vectors = [att("maa_x"), att("maa_w"), att("maa_k"), att("maa_v"), att("maa_r"), att("maa_g"),
               att("time_decay"), att("u").reshape(-1)]
    arrays = {
        "x": att("x").reshape(T, D),
        "rwT": ffn("router_w").T,
        "rb": ffn("router_b"),
        "w1": ffn("w1"),
        "b1T": ffn("b1").reshape(E, FC, P).transpose(2, 0, 1).reshape(P, E * FC),
        "w2": ffn("w2"),
        "b2": ffn("b2").reshape(E * D),
        "chvec": np.stack(vectors).reshape(8, DC, P).transpose(2, 0, 1),
        "maa_w1": att("maa_w1"),
        "maa_w2": att("maa_w2").reshape(160, D),
        "Wr": att("Wr"), "Wk": att("Wk"), "Wv": att("Wv"), "Wo": att("Wo"),
        "gw1": att("gate_w1"), "gw2": att("gate_w2"), "dw1": att("decay_w1"), "dw2": att("decay_w2"),
        "ln_g": att("ln_g"), "ln_b": att("ln_b"),
    }
    arrays = {"in_" + k: np.ascontiguousarray(a) for k, a in arrays.items()}
    nc = bacc.Bacc("TRN2", target_bir_lowering=False, num_devices=1)
    args = [nc.dram_tensor(k, a.shape, mybir.dt.from_np(a.dtype), kind="ExternalInput").ap()
            for k, a in arrays.items()]
    out = nc.dram_tensor("out", (T, D), F32, kind="ExternalOutput").ap()
    program(nc, *args, out, DEBUG)
    r = run_bass_kernel_spmd(nc, [arrays], core_ids=[0])
    return r.results[0]["out"].reshape(T // SEQ, SEQ, D)
```

```python
import concourse.bass as bass
from concourse import mybir
from contextlib import ExitStack

F32 = mybir.dt.float32
F32R = mybir.dt.float32r
U32 = mybir.dt.uint32
ALU = mybir.AluOpType
ACT = mybir.ActivationFunctionType
AX = mybir.AxisListType

P = 128
T = 8192
SEQ = 1024
D = 256
DC = D // P
E = 16
TOPK = 2
CAP = 1280
DFF = 1024
FC = DFF // P
NT = T // P
GQ = 4
NG = NT // GQ
GT = GQ * P
BS = 256
NB = CAP // BS
H = 4
N = 64
LEVELS = 7
SKIP = 1 << 20


def due(value):
    return not isinstance(value, int) or value > 0


def loop(eng, count, step):
    step(0)
    with eng.Fori(1, count) as i:
        step(i)


def loop_with_last(eng, count, step):
    step(0, False)
    with eng.Fori(1, count - 1) as i:
        step(i, False)
    step(count - 1, True)


class Chain:

    def __init__(self, eng, sem, base=0):
        self.eng, self.sem, self.base, self.n = eng, sem, base, 0

    def __call__(self, ins):
        ins.then_inc(self.sem, 1)
        self.n += 1

    def settle(self):
        self.eng.wait_ge(self.sem, self.base + self.n)


def constants(nc, S):
    done, made, zeroed = S.sem("const_loaded"), S.sem("const_made"), S.sem("const_zeroed")
    with nc.Block() as block:
        @block.sync
        def _(sp):
            n = 0
            for dst, src in S.loads:
                sp.dma_start(dst, src).then_inc(done, 16)
                n += 16
            sp.wait_ge(done, n)
            sp.wait_ge(zeroed, 1)

        @block.vector
        def _(dve):
            dve.memset(S.zeros[:, :], 0.0).then_inc(zeroed, 1)

        @block.gpsimd
        def _(pool):
            c = Chain(pool, made)
            c(pool.memset(S.ones[:, :], 1.0))
            c(pool.memset(S.eps[:, 0:1], 1e-5))
            c(pool.memset(S.gidx[:, NT:, :], 0))
            c(pool.memset(S.eps[:, 1:2], 0.00064))
            c(pool.memset(S.ident[:, :], 0.0))
            c(pool.memset(S.before[:, :], 1.0))
            c(pool.iota(S.iota_i[:, :], pattern=[[1, E]], base=0, channel_multiplier=0))
            c.settle()
            c(pool.tensor_copy(S.iota_f[:, :], S.iota_i[:, :]))
            c(pool.affine_select(out=S.ident[:, :], in_=S.ident[:, :], compare_op=ALU.not_equal, fill=1.0,
                                 base=0, pattern=[[-1, P]], channel_multiplier=1))
            c(pool.affine_select(out=S.before[:, :], in_=S.before[:, :], compare_op=ALU.is_gt, fill=0.0,
                                 base=0, pattern=[[1, P]], channel_multiplier=-1))
            c.settle()


def level_masks(nc, S):
    made = S.sem("masks_made")
    with ExitStack() as ctx, nc.Block() as block:
        s_i = ctx.enter_context(nc.sbuf_tensor("mask_s", [P, N], mybir.dt.int32))
        t_i = ctx.enter_context(nc.sbuf_tensor("mask_t", [P, N], mybir.dt.int32))
        a_i = ctx.enter_context(nc.sbuf_tensor("mask_a", [P, 4, N], mybir.dt.int32))
        f_i = ctx.enter_context(nc.sbuf_tensor("mask_f", [P, 3, N], F32))
        iot = S.sem("mask_iota")

        @block.gpsimd
        def _(pool):
            pool.iota(s_i[:, :], pattern=[[0, N]], base=0, channel_multiplier=1).then_inc(iot, 1)
            pool.iota(t_i[:, :], pattern=[[1, N]], base=0, channel_multiplier=0).then_inc(iot, 1)

        @block.vector
        def _(dve):
            c = Chain(dve, made)
            dve.wait_ge(iot, 2)
            for l in range(6):
                c(dve.tensor_scalar(a_i[:, 0], s_i[:, :], l + 1, (N >> (l + 1)) - 1,
                                    ALU.logical_shift_right, ALU.bitwise_and))
                c(dve.tensor_scalar(a_i[:, 1], t_i[:, :], l + 1, None, ALU.logical_shift_right))
                c(dve.tensor_scalar(a_i[:, 2], s_i[:, :], l, 1, ALU.logical_shift_right, ALU.bitwise_and))
                c(dve.tensor_scalar(a_i[:, 3], t_i[:, :], l, 1, ALU.logical_shift_right, ALU.bitwise_and))
                c.settle()
                c(dve.tensor_tensor(f_i[:, 0], a_i[:, 0], a_i[:, 1], ALU.is_equal))
                c(dve.tensor_tensor(f_i[:, 1], a_i[:, 3], a_i[:, 2], ALU.is_gt))
                c.settle()
                c(dve.tensor_tensor(S.lev[:, l, :], f_i[:, 0], f_i[:, 1], ALU.mult))
                c.settle()
            c(dve.tensor_scalar(a_i[:, 0], s_i[:, :], N - 1, None, ALU.bitwise_and))
            c.settle()
            c(dve.tensor_tensor(S.diag[:, :], a_i[:, 0], t_i[:, :], ALU.is_equal))
            c.settle()


def layer_norm(dve, c, S, st, mv, rstd, rstd_at, x_tiles, out_tiles, ready):
    for q in range(GQ):
        c(dve.bn_stats(st[:, q, :], x_tiles(q)))
    c.settle()
    S.apart(dve)
    for q in range(GQ):
        c(dve.bn_aggr(mv[:, q, :], st[:, q, :]))
    c.settle()
    dve.sem_inc(S.var_ready, 1)
    dve.wait_ge(S.rstd_ready, rstd_at)
    c(dve.reciprocal(rstd, rstd))
    c.settle()
    for q in range(GQ):
        ins = dve.tensor_scalar(out_tiles(q), x_tiles(q), mv[:, q, 0:1], rstd[:, q:q + 1],
                                ALU.subtract, ALU.mult)
        if q < GQ - 1:
            c(ins)
    ins.then_inc(ready, 1)


def root(act, S, var, eps, out, at):
    act.wait_ge(S.var_ready, at)
    act.activation(out, var, ACT.Sqrt, bias=eps).then_inc(S.rstd_ready, 1)


def route(nc, S, tag):
    PER = 76
    with ExitStack() as ctx:
        def sb(name, shape, dt=F32):
            return ctx.enter_context(nc.sbuf_tensor(f"{tag}r_{name}", shape, dt))

        def ps(name, shape):
            return ctx.enter_context(nc.psum_tensor(f"{tag}r_{name}", shape, F32))

        def sem(name):
            return S.sem(f"{tag}_{name}")

        xn = [sb(f"xn{u}", [P, GQ, D]) for u in range(4)]
        xT = [sb(f"xT{u}", [P, DC, GT]) for u in range(2)]
        st = sb("st", [P, 2, GQ, 6])
        mv = sb("mv", [P, 2, GQ, 2])
        rstd = sb("rstd", [P, 2, GQ])
        logit = [sb(f"logit{u}", [P, GQ, E]) for u in range(2)]
        top = [sb(f"top{u}", [P, GQ, 8]) for u in range(2)]
        topi = [sb(f"topi{u}", [P, GQ, 8], U32) for u in range(2)]
        ef = [sb(f"ef{u}", [P, GQ, TOPK]) for u in range(2)]
        oh = [sb(f"oh{u}", [P, GQ * TOPK, E]) for u in range(2)]
        cnt = [sb(f"cnt{u}", [P, GQ, E]) for u in range(2)]
        sumc = sb("sumc", [P, E])
        seen = [sb(f"seen{u}", [P, E]) for u in range(2)]
        pex = [sb(f"pex{u}", [P, GQ * TOPK, E]) for u in range(2)]
        pos = [sb(f"pos{u}", [P, GQ, TOPK]) for u in range(2)]
        slot = [sb(f"slot{u}", [P, GQ, TOPK]) for u in range(2)]
        kept = [sb(f"kept{u}", [P, GQ, TOPK]) for u in range(2)]
        over = [sb(f"over{u}", [P, GQ, TOPK]) for u in range(2)]
        sidx = [sb(f"sidx{u}", [P, GQ, TOPK], U32) for u in range(4)]
        dif = [sb(f"dif{u}", [P, GQ]) for u in range(2)]
        ex = [sb(f"ex{u}", [P, GQ]) for u in range(2)]
        gt = [sb(f"gt{u}", [P, GQ, TOPK]) for u in range(2)]
        den = [sb(f"den{u}", [P, GQ]) for u in range(2)]
        pT = [ps(f"pT{c}", [P, GT]) for c in range(DC)]
        bank = [ps(f"bank{k}", [P, GT]) for k in range(4)]
        pL, pC = ([bank[k + u][:, 0:GQ * E].rearrange("p (q e) -> p q e", e=E) for u in range(2)] for k in (0, 2))

        x_loaded = [sem(f"x_loaded{u}") for u in range(2)]
        xn_ready = sem("xn_ready")
        transposed = sem("transposed")
        xT_ready = sem("xT_ready")
        logits_ready = sem("logits_ready")
        counts_ready = sem("counts_ready")
        seen_ready = sem("seen_ready")
        prefix_ready = sem("prefix_ready")
        dif_ready = sem("dif_ready")
        ex_ready = sem("ex_ready")
        sidx_ready = sem("sidx_ready")
        scattered = [sem(f"scattered{u}") for u in range(4)]
        chain = sem("route_chain")
        x_grp = S.x.rearrange("(g q p) d -> g p q d", p=P, q=GQ)

        with nc.Block() as block:
            if tag == "a":
                @block.sync
                def _(sp):
                    def fill():
                        rows = S.slots.rearrange("(a p b) d -> a p (b d)", p=P, b=10)
                        for a in range(16):
                            sp.dma_start(rows[a], S.zeros[:, :]).then_inc(S.slots_zeroed, 16)

                    def step(o):
                        for pr in range(2):
                            i = o * 2 + pr
                            for u in range(2):
                                if due(i * 16):
                                    sp.wait_ge(x_loaded[u], i * 16)
                                sp.dma_start(S.x_sb[:, bass.ds((i * 2 + u) * GQ, GQ), :],
                                             x_grp[i * 2 + u]).then_inc(x_loaded[u], 16)
                            if isinstance(o, int) and pr == 0:
                                fill()
                    loop(sp, NG // 4, step)

            @block.vector
            def _(dve):
                dve.memset(seen[0][:, :], 0.0).then_inc(seen_ready, 1)
                def step(o):
                    for pr in range(2):
                        i = o * 2 + pr
                        c = Chain(dve, chain, i * PER)
                        for u in range(2):
                            if tag == "a":
                                dve.wait_ge(x_loaded[u], i * 16 + 16)
                            if due(o * (16 * GQ * TOPK)):
                                dve.wait_ge(scattered[2 * pr + u], o * (16 * GQ * TOPK))
                            if due(i * 2):
                                dve.wait_ge(transposed, i * 2)
                            layer_norm(dve, c, S, st[:, u], mv[:, u], rstd[:, u, :], i * 2 + (u + 1 + S.n_roots[tag]),
                                       lambda q: S.x_sb[:, (i * 2 + u) * GQ + q, :],
                                       lambda q: xn[2 * pr + u][:, q, :], xn_ready)
                        for u in range(2):
                            dve.wait_ge(logits_ready, i * 2 + u + 1)
                            c(dve.tensor_tensor(logit[u][:, :, :], pL[u][:, :, :],
                                                S.rb[:, :].unsqueeze(1).to_broadcast([P, GQ, E]), ALU.add))
                            c.settle()
                            S.apart(dve)
                            for q in range(GQ):
                                c(dve.max(top[u][:, q, :], logit[u][:, q, :]))
                            c.settle()
                            S.apart(dve)
                            for q in range(GQ):
                                c(dve.max_index(topi[u][:, q, :], top[u][:, q, :], logit[u][:, q, :]))
                            if due(i * 2 + u):
                                dve.wait_ge(ex_ready, i * 2 + u)
                            dve.tensor_tensor(dif[u][:, :], top[u][:, :, 1], top[u][:, :, 0],
                                              ALU.subtract).then_inc(dif_ready, 1)
                            c.settle()
                            c(dve.tensor_copy(ef[u][:, :, :], topi[u][:, :, 0:TOPK]))
                            c.settle()
                            c(dve.tensor_tensor(
                                oh[u][:, :, :],
                                S.iota_f[:, :].unsqueeze(1).to_broadcast([P, GQ * TOPK, E]),
                                ef[u][:, :, :].rearrange("p q k -> p (q k)").unsqueeze(2).to_broadcast([P, GQ * TOPK, E]),
                                ALU.is_equal))
                            c.settle()
                            ohk = oh[u][:, :, :].rearrange("p (q k) e -> p q k e", k=TOPK)
                            if due(i * 2):
                                dve.wait_ge(prefix_ready, i * 2)
                            dve.tensor_tensor(cnt[u][:, :, :], ohk[:, :, 0, :], ohk[:, :, 1, :],
                                              ALU.add).then_inc(counts_ready, 1)
                            dve.wait_ge(counts_ready, i * 2 + u + 1)
                            c(dve.tensor_reduce(sumc[:, :], cnt[u][:, :, :].rearrange("p q e -> p e q"),
                                                AX.X, ALU.add))
                            c.settle()
                            if u == 1:
                                dve.wait_ge(prefix_ready, i * 2 + 1)
                            dve.wait_ge(seen_ready, i * 2 + u + 1)
                            dve.tensor_tensor(seen[1 - u][:, :], seen[u][:, :], sumc[:, :],
                                              ALU.add).then_inc(seen_ready, 1)
                        for u in range(2):
                            dve.wait_ge(prefix_ready, i * 2 + u + 1)
                            pexk = pex[u][:, :, :].rearrange("p (q k) e -> p q k e", k=TOPK)
                            ohk = oh[u][:, :, :].rearrange("p (q k) e -> p q k e", k=TOPK)
                            c(dve.tensor_tensor(pexk, ohk, pC[u][:, :, :].unsqueeze(2).to_broadcast([P, GQ, TOPK, E]),
                                                ALU.mult))
                            c.settle()
                            c(dve.tensor_reduce(pos[u][:, :, :].rearrange("p q k -> p (q k)"), pex[u][:, :, :],
                                                AX.X, ALU.add))
                            c.settle()
                            c(dve.tensor_scalar(kept[u][:, :, :], pos[u][:, :, :], float(CAP), None, ALU.is_lt))
                            c(dve.tensor_scalar(over[u][:, :, :], pos[u][:, :, :], float(CAP), float(SKIP),
                                                ALU.is_ge, ALU.mult))
                            c(dve.scalar_tensor_tensor(out=slot[u][:, :, :], in0=ef[u][:, :, :], scalar=float(CAP),
                                                       in1=pos[u][:, :, :], op0=ALU.mult, op1=ALU.add))
                            c.settle()
                            dve.tensor_tensor(sidx[2 * pr + u][:, :, :], slot[u][:, :, :], over[u][:, :, :],
                                              ALU.add).then_inc(sidx_ready, 1)
                            c(dve.tensor_scalar(S.gidx[:, bass.ds((i * 2 + u) * GQ, GQ), :], slot[u][:, :, :],
                                                float(E * CAP - 1), None, ALU.min))
                            dve.wait_ge(ex_ready, i * 2 + u + 1)
                            c(dve.tensor_scalar(den[u][:, :], ex[u][:, :], 1.0, None, ALU.add))
                            c.settle()
                            c(dve.reciprocal(gt[u][:, :, 0], den[u][:, :]))
                            c.settle()
                            c(dve.tensor_tensor(gt[u][:, :, 1], gt[u][:, :, 0], ex[u][:, :], ALU.mult))
                            c.settle()
                            c(dve.tensor_tensor(gt[u][:, :, :], gt[u][:, :, :], kept[u][:, :, :], ALU.mult))
                            c.settle()
                            c(dve.scalar_tensor_tensor(out=den[u][:, :], in0=gt[u][:, :, 0], scalar=1e-9,
                                                       in1=gt[u][:, :, 1], op0=ALU.add, op1=ALU.add))
                            c.settle()
                            c(dve.reciprocal(den[u][:, :], den[u][:, :]))
                            c.settle()
                            c(dve.tensor_scalar(den[u][:, :], den[u][:, :], 0.5, None, ALU.mult))
                            c.settle()
                            c(dve.tensor_tensor(S.gw[:, bass.ds((i * 2 + u) * GQ, GQ), :], gt[u][:, :, :],
                                                den[u][:, :].unsqueeze(2).to_broadcast([P, GQ, TOPK]), ALU.mult))
                        S.check(c.n, PER, tag + "route")
                loop(dve, NG // 4, step)

            @block.tensor
            def _(pe):
                def step(o):
                    for pr in range(2):
                        i = o * 2 + pr
                        for u in range(2):
                            pe.wait_ge(xn_ready, i * 2 + u + 1)
                            if due(i * 2 + u):
                                pe.wait_ge(xT_ready, i * 2 + u)
                            for q in range(GQ):
                                for k in range(DC):
                                    t = pe.transpose(pT[k][:, q * P:(q + 1) * P], xn[2 * pr + u][:, q, k * P:(k + 1) * P],
                                                     S.ident[:, :])
                            t.then_inc(transposed, 1)
                        for u in range(2):
                            pe.wait_ge(xT_ready, i * 2 + u + 1)
                            for q in range(GQ):
                                for k in range(DC):
                                    t = pe.matmul(pL[u][:, q, :], xT[u][:, k, q * P:(q + 1) * P], S.rwT[:, k, :],
                                                  start=(k == 0), stop=(k == DC - 1))
                            t.then_inc(logits_ready, 1)
                        for u in range(2):
                            pe.wait_ge(counts_ready, i * 2 + u + 1)
                            pe.wait_ge(seen_ready, i * 2 + u + 1)
                            pe.matmul(pC[u][:, :, :], S.before[:, :], cnt[u][:, :, :], start=True, stop=False)
                            for j in range(GQ - 1):
                                pe.matmul(pC[u][:, j + 1:, :], S.ones[:, :],
                                          cnt[u][:, j:j + 1, :].to_broadcast([P, GQ - 1 - j, E]),
                                          start=False, stop=False)
                            pe.matmul(pC[u][:, :, :], S.ones[:, :],
                                      seen[u][:, :].unsqueeze(1).to_broadcast([P, GQ, E]),
                                      start=False, stop=True).then_inc(prefix_ready, 1)
                loop(pe, NG // 4, step)

            @block.scalar
            def _(act):
                def step(o):
                    for pr in range(2):
                        i = o * 2 + pr
                        for u in range(2):
                            root(act, S, mv[:, u, :, 1], S.eps[:, 0:1], rstd[:, u], i * 2 + (u + 1 + S.n_roots[tag]))
                        for u in range(2):
                            act.wait_ge(transposed, i * 2 + u + 1)
                            if due(i * 2):
                                act.wait_ge(logits_ready, i * 2)
                            act.copy(xT[u][:, 0, :], pT[0][:, :])
                            act.copy(xT[u][:, 1, :], pT[1][:, :]).then_inc(xT_ready, 1)
                        for u in range(2):
                            act.wait_ge(dif_ready, i * 2 + u + 1)
                            act.activation(ex[u][:, :], dif[u][:, :], ACT.Exp).then_inc(ex_ready, 1)
                loop(act, NG // 4, step)

            @block.gpsimd
            def _(pool):
                pool.wait_ge(S.slots_zeroed, 16 * 16)
                def step(o):
                    for pr in range(2):
                        i = o * 2 + pr
                        for u in range(2):
                            pool.wait_ge(xn_ready, i * 2 + u + 1)
                            pool.wait_ge(sidx_ready, i * 2 + u + 1)
                            S.apart(pool)
                            for q in range(GQ):
                                for k in range(TOPK):
                                    pool.indirect_dma_start(
                                        S.slots[:, :], bass.IndirectOffsetOnAxis(ap=sidx[2 * pr + u][:, q, k:k + 1], axis=0),
                                        xn[2 * pr + u][:, q, :], None, bounds_check=E * CAP - 1,
                                        oob_is_err=False).then_inc(scattered[2 * pr + u], 16)
                loop(pool, NG // 4, step)
                for u in range(4):
                    pool.wait_ge(scattered[u], NG // 4 * 16 * GQ * TOPK)


def experts(nc, S, tag):
    with ExitStack() as ctx:
        def sb(name, shape, dt=F32):
            return ctx.enter_context(nc.sbuf_tensor(f"{tag}e_{name}", shape, dt))

        def ps(name, shape):
            return ctx.enter_context(nc.psum_tensor(f"{tag}e_{name}", shape, F32))

        def sem(name):
            return S.sem(f"{tag}_{name}")

        HI, LO = 0, 1
        XR = 2
        M = 2 * NB
        HB = FC // 2
        WP = 4
        stage = [sb(f"stage{k}", [P, DFF]) for k in range(2)]
        w1 = [[sb(f"w1_{u}{k}", [P, DC, DFF], F32R) for k in "hl"] for u in range(2)]
        w2 = [[sb(f"w2_{u}{k}", [P, FC, D], F32R) for k in "hl"] for u in range(2)]
        b2 = [sb(f"b2_{u}", [P, D]) for u in range(2)]
        xp = [sb(f"xp{b}", [P, 2, D]) for b in range(XR)]
        xT = [[sb(f"xT{r}{k}", [P, DC, BS], F32R) for k in "hl"] for r in range(2)]
        h32 = sb("h32", [P, FC, BS])
        hT = [[sb(f"hT{r}{k}", [P, FC, BS], F32R) for k in "hl"] for r in range(2)]
        ob = [sb(f"ob{r}", [P, 2, D]) for r in range(2)]
        pT = [ps(f"pT{r}", [P, DC, BS]) for r in range(2)]
        pH = ps("pH", [P, FC, BS])
        pO = [ps(f"pO{r}", [P, 2, D]) for r in range(2)]

        w_loaded = [sem(f"w_loaded{k}") for k in range(2)]
        w_high = [sem(f"w_high{k}") for k in range(2)]
        w_split = [sem(f"w_split{k}") for k in range(2)]
        b2_loaded = [sem(f"b2_loaded{u}") for u in range(2)]
        xp_loaded = [sem(f"xp_loaded{b}") for b in range(XR)]
        xp_used = [sem(f"xp_used{b}") for b in range(XR)]
        xT_high = [sem(f"exT_high{r}") for r in range(2)]
        xT_ready = [sem(f"exT_ready{r}") for r in range(2)]
        up_full = [sem(f"up_full{h}") for h in range(HB)]
        gelu_done = [sem(f"gelu_done{h}") for h in range(HB)]
        h_split = [sem(f"h_split{h}") for h in range(HB)]
        down_done = [sem(f"down_done{r}") for r in range(2)]
        out_ready = [sem(f"out_ready{r}") for r in range(2)]
        stored = [sem(f"stored{r}") for r in range(2)]

        w1_d = S.w1.rearrange("e (c p) f -> e p c f", p=P)
        w2_d = S.w2.rearrange("e (c p) d -> e p c d", p=P)
        xp_d = S.slots.rearrange("(n q p) d -> n p q d", p=P, q=2)
        eo_d = S.eout.rearrange("(n q p) d -> n p q d", p=P, q=2)

        def half(i, m):
            return i * (M // 2) + m // 2

        def part(i, u, k):
            return i * 4 + (2 * u + k // 2)

        def whole(u, k, side):
            if k < 2:
                return w1[u % 2][side][:, k, :]
            return w2[u % 2][side][:, (k - 2) * 4:(k - 1) * 4, :].rearrange("p c d -> p (c d)")

        def hidden(t, h):
            return t[:, 2 * h:2 * h + 2, :].rearrange("p c s -> p (c s)")

        with nc.Block() as block:
            @block.sync
            def _(sp):
                def weights(i, u, k):
                    if due(part(i, u, k)):
                        sp.wait_ge(w_split[k % 2], part(i, u, k))
                    e = i * 2 + u
                    if k < 2:
                        src, dst = w1_d[e][:, k, :], stage[k % 2][:, :]
                    else:
                        src = w2_d[e][:, (k - 2) * 4:(k - 1) * 4, :]
                        dst = stage[k % 2][:, :].rearrange("p (c d) -> p c d", d=D)
                    sp.dma_start(dst, src).then_inc(w_loaded[k % 2], 16)

                for k in range(WP):
                    weights(0, 0, k)

                def step(i, last):
                    for m in range(M):
                        u, b = m // NB, m % NB
                        if due(half(i, m)):
                            sp.wait_ge(xp_used[m % XR], half(i, m))
                        sp.dma_start(xp[m % XR][:, :, :], xp_d[i * M + m]).then_inc(xp_loaded[m % XR], 16)
                        if b == 0:
                            o = m + NB - 1
                            if due(half(i, o) + 1 - M // 2):
                                sp.wait_ge(out_ready[o % 2], half(i, o) + 1 - M // 2)
                            sp.dma_start(b2[u][:, :], S.b2[i * 2 + u].partition_broadcast(P)).then_inc(b2_loaded[u], 16)
                        if b < WP and not (last and u == 1):
                            weights(i, u + 1, b)

                loop_with_last(sp, E // 2, step)

            @block.tensor
            def _(pe):
                def turn(i, m):
                    pe.wait_ge(xp_loaded[m % XR], half(i, m) * 16 + 16)
                    if due(half(i, m)):
                        pe.wait_ge(xT_ready[m % 2], half(i, m))
                    for q in range(2):
                        for k in range(DC):
                            t = pe.transpose(pT[m % 2][:, k, q * P:(q + 1) * P], xp[m % XR][:, q, k * P:(k + 1) * P],
                                             S.ident[:, :])
                    t.then_inc(xp_used[m % XR], 1)

                passes = [(HI, HI), (HI, LO), (LO, HI)]

                def up(i, m):
                    u = m // NB
                    pe.wait_ge(xT_ready[m % 2], half(i, m) + 1)
                    if m % NB == 0:
                        for k in range(2):
                            pe.wait_ge(w_split[k], part(i, u, 2 + k) + 1)
                    for f in range(FC):
                        if f % 2 == 0:
                            if due(i * M + m):
                                pe.wait_ge(gelu_done[f // 2], i * M + m)
                        n = 0
                        for k in range(DC):
                            for a, b in passes:
                                t = pe.matmul(pH[:, f, :], w1[u][a][:, k, f * P:(f + 1) * P], xT[m % 2][b][:, k, :],
                                              start=(n == 0), stop=(n == 3 * DC - 1), skip_group_check=True)
                                n += 1
                        if f % 2:
                            t.then_inc(up_full[f // 2], 1)

                def down(i, m):
                    u = m // NB
                    if due(half(i, m)):
                        pe.wait_ge(out_ready[m % 2], half(i, m))
                    for h in range(HB):
                        pe.wait_ge(h_split[h], i * M + (m + 1))
                    for q in range(2):
                        n = 0
                        for f in range(FC):
                            for a, b in passes:
                                t = pe.matmul(pO[m % 2][:, q, :], hT[m % 2][a][:, f, q * P:(q + 1) * P], w2[u][b][:, f, :],
                                              start=(n == 0), stop=(n == 3 * FC - 1))
                                n += 1
                    t.then_inc(down_done[m % 2], 1)

                def step(i):
                    turn(i, 0)
                    for m in range(M):
                        up(i, m)
                        if m + 1 < M:
                            turn(i, m + 1)
                        if m:
                            down(i, m - 1)
                    down(i, M - 1)

                loop(pe, E // 2, step)

            @block.scalar
            def _(act):
                def step(i):
                    def store(m):
                        act.wait_ge(out_ready[m % 2], half(i, m) + 1)
                        act.dma_start(eo_d[i * M + m], ob[m % 2][:, :, :]).then_inc(stored[m % 2], 16)

                    for m in range(M):
                        if due(half(i, m)):
                            act.wait_ge(down_done[m % 2], half(i, m))
                        for f in range(FC):
                            if f % 2 == 0:
                                if due(i * M + m):
                                    act.wait_ge(h_split[f // 2], i * M + m)
                                act.wait_ge(up_full[f // 2], i * M + (m + 1))
                                S.apart(act)
                            for dst in (h32, hT[m % 2][HI]):
                                t = act.activation(dst[:, f, :], pH[:, f, :], ACT.Gelu,
                                                   bias=S.b1[:, bass.ds(i * (2 * FC) + ((m // NB) * FC + f), 1)])
                            if f % 2:
                                t.then_inc(gelu_done[f // 2], 1)
                        if m:
                            store(m - 1)
                    store(M - 1)

                loop(act, E // 2, step)
                for r in range(2):
                    act.wait_ge(stored[r], E // 2 * (M // 2) * 16)

            @block.gpsimd
            def _(pool):
                def weights_high(i, u, k):
                    pool.wait_ge(w_loaded[k % 2], part(i, u, k) * 16 + 16)
                    S.apart(pool)
                    pool.tensor_copy(whole(u, k, HI), stage[k % 2][:, :]).then_inc(w_high[k % 2], 1)

                for k in range(WP):
                    weights_high(0, 0, k)

                def step(i, last):
                    for m in range(M):
                        if m % NB < WP and not (last and m >= NB):
                            before = m - m % NB - 1
                            if due(half(i, before) + 1):
                                pool.wait_ge(down_done[before % 2], half(i, before) + 1)
                            weights_high(i, m // NB + 1, m % NB)

                loop_with_last(pool, E // 2, step)

            @block.vector
            def _(dve):
                def weights_low(i, u, k):
                    dve.wait_ge(w_high[k % 2], part(i, u, k) + 1)
                    dve.tensor_tensor(whole(u, k, LO), stage[k % 2][:, :], whole(u, k, HI),
                                      ALU.subtract).then_inc(w_split[k % 2], 1)

                def turned(i, m):
                    dve.wait_ge(xp_used[m % XR], half(i, m) + 1)
                    if due(i * M + max(m - 1, 0)):
                        dve.wait_ge(up_full[HB - 1], i * M + max(m - 1, 0))
                    dve.tensor_copy(xT[m % 2][HI][:, :, :], pT[m % 2][:, :, :]).then_inc(xT_high[m % 2], 1)
                    dve.wait_ge(xT_high[m % 2], half(i, m) + 1)
                    dve.tensor_tensor(xT[m % 2][LO][:, :, :], pT[m % 2][:, :, :], xT[m % 2][HI][:, :, :],
                                      ALU.subtract).then_inc(xT_ready[m % 2], 1)

                def out(i, m):
                    dve.wait_ge(down_done[m % 2], half(i, m) + 1)
                    if due(half(i, m) * 16):
                        dve.wait_ge(stored[m % 2], half(i, m) * 16)
                    if m % NB == 0:
                        dve.wait_ge(b2_loaded[m // NB], i * 16 + 16)
                    dve.tensor_tensor(ob[m % 2][:, :, :], pO[m % 2][:, :, :],
                                      b2[m // NB][:, :].unsqueeze(1).to_broadcast([P, 2, D]),
                                      ALU.add).then_inc(out_ready[m % 2], 1)

                for k in range(WP):
                    weights_low(0, 0, k)

                def step(i, last):
                    turned(i, 0)
                    for m in range(M):
                        if due(half(i, m)):
                            dve.wait_ge(down_done[m % 2], half(i, m))
                        for h in range(HB):
                            dve.wait_ge(gelu_done[h], i * M + (m + 1))
                            dve.tensor_tensor(hidden(hT[m % 2][LO], h), hidden(h32, h), hidden(hT[m % 2][HI], h),
                                              ALU.subtract).then_inc(h_split[h], 1)
                        if m + 1 < M:
                            turned(i, m + 1)
                        if m:
                            out(i, m - 1)
                        if m % NB < WP and not (last and m >= NB):
                            weights_low(i, m // NB + 1, m % NB)
                    out(i, M - 1)

                loop_with_last(dve, E // 2, step)


def combine(nc, S, tag):
    with ExitStack() as ctx:
        CB = 4
        rows = [ctx.enter_context(nc.sbuf_tensor(f"{tag}c_rows{u}", [P, GQ, TOPK, D], F32)) for u in range(CB)]
        idx = [ctx.enter_context(nc.sbuf_tensor(f"{tag}c_idx{u}", [P, GQ, TOPK], U32)) for u in range(CB)]
        idx_ready = S.sem(f"{tag}_idx_ready")
        gathered = [S.sem(f"{tag}_gathered{u}") for u in range(CB)]
        first = S.sem(f"{tag}_first_added")
        added = S.sem(f"{tag}_added")
        out_stored = S.sem(f"{tag}_out_stored")
        o_grp = S.out.rearrange("(g q p) d -> g p q d", p=P, q=GQ)
        with nc.Block() as block:
            @block.vector
            def _(dve):
                def prepare(i, u):
                    dve.tensor_copy(idx[u][:, :, :],
                                    S.gidx[:, bass.ds((i * CB + u) * GQ, GQ), :]).then_inc(idx_ready, 1)

                def step(i, last):
                    for u in range(CB):
                        dve.wait_ge(gathered[u], i * (16 * GQ * TOPK) + 16 * GQ * TOPK)
                        for k in range(TOPK):
                            if k:
                                dve.wait_ge(first, i * (CB * GQ) + (u * GQ + GQ))
                            for q in range(GQ):
                                x = S.x_sb[:, (i * CB + u) * GQ + q, :]
                                t = dve.scalar_tensor_tensor(
                                    out=x, in0=rows[u][:, q, k, :], scalar=S.gw[:, (i * CB + u) * GQ + q, k:k + 1],
                                    in1=x, op0=ALU.mult, op1=ALU.add)
                                t.then_inc(first if k == 0 else added, 1)
                        if not last:
                            prepare(i + 1, u)

                for u in range(CB):
                    prepare(0, u)
                loop_with_last(dve, NG // CB, step)

            @block.gpsimd
            def _(pool):
                def step(i):
                    for u in range(CB):
                        pool.wait_ge(idx_ready, i * CB + u + 1)
                        if not isinstance(i, int):
                            pool.wait_ge(added, (i - 1) * (CB * GQ) + (u + 1) * GQ)
                        S.apart(pool)
                        for q in range(GQ):
                            for k in range(TOPK):
                                pool.indirect_dma_start(
                                    rows[u][:, q, k, :], None, S.eout[:, :],
                                    bass.IndirectOffsetOnAxis(ap=idx[u][:, q, k:k + 1], axis=0)
                                ).then_inc(gathered[u], 16)
                loop(pool, NG // CB, step)

            @block.sync
            def _(sp):
                def step(g):
                    sp.wait_ge(added, g * GQ + GQ)
                    sp.dma_start(o_grp[g], S.x_sb[:, bass.ds(g * GQ, GQ), :]).then_inc(out_stored, 16)
                loop(sp, NG, step)
                sp.wait_ge(out_stored, NG * 16)


def mix(nc, S):
    NJ = 36
    NBK = 4
    with ExitStack() as ctx:
        def sb(name, shape, dt=F32):
            return ctx.enter_context(nc.sbuf_tensor(f"m_{name}", shape, dt))

        def sem(name):
            return S.sem(f"m_{name}")

        st = sb("st", [P, GQ, 6])
        mv = sb("mv", [P, GQ, 2])
        rstd = sb("rstd", [P, GQ])
        xT = sb("xT", [P, DC, GT + 1])
        xx = sb("xx", [P, DC, GT])
        xxx = sb("xxx", [P, DC, GT])
        lora = sb("lora", [P, GT])
        lorag = sb("lorag", [32, GT])
        tmp = [sb(f"tmp{j}", [P, GT]) for j in range(2)]
        xf = [sb(f"xf{f}", [P, DC, GT]) for f in range(5)]
        tw = sb("tw", [N, GT])
        tg = sb("tg", [N, GT])
        W = sb("W", [P, DC * GT])
        tot = [W] + [sb(f"tot{l}", [P, DC * GT >> l]) for l in range(1, LEVELS + 1)]
        RP = sb("RP", [P, DC, GT])
        KS = sb("KS", [P, DC, GT])
        V = sb("V", [P, GQ, D])
        G = sb("G", [P, GQ, D])
        A = sb("A", [P, 2 * GQ * 2, N])
        Af = sb("Af", [P, 2 * GQ * 2, P])
        KR = sb("KR", [P, GQ, D])
        Sbd = sb("Sbd", [P, 2, P])
        Y = sb("Y", [P, GQ, D])
        Y2 = sb("Y2", [P, GQ, D])
        xn = Y2
        RU = Y[:, :, :].rearrange("p (c a) d -> p c (a d)", c=DC)
        mean = sb("mean", [P, GQ * H])
        var = sb("var", [P, GQ * H])
        rvar = sb("rvar", [P, GQ * H])
        ygT = KR[:, :, :].rearrange("p (c a) d -> p c (a d)", c=DC)
        B = [ctx.enter_context(nc.psum_tensor(f"m_B{k}", [P, GT], F32)) for k in range(NBK)]
        PX = ctx.enter_context(nc.psum_tensor("m_PX", [P, 2, GT], F32))
        PA = ctx.enter_context(nc.psum_tensor("m_PA", [P, 2, GT], F32))

        S.lev = sb("lev", [P, 6, N], mybir.dt.int32)
        S.diag = sb("diag", [P, N])
        level_masks(nc, S)
        PP = [PX, PA]

        filled = [sem(f"filled{k}") for k in range(NBK)]
        drained = [sem(f"drained{k}") for k in range(NBK)]
        fetched = [sb(f"fetched{u}", [P, GQ, TOPK, D]) for u in range(2)]
        idx = [sb(f"idx{u}", [P, GQ, TOPK], U32) for u in range(2)]
        idx_ready = sem("idx_ready")
        gathered = [sem(f"gathered{u}") for u in range(2)]
        weights_loaded = sem("weights_loaded")
        S.ch = sb("ch", [P, 8, DC])
        S.maa_w1 = sb("maa_w1", [P, DC, 160])
        S.maa_w2 = sb("maa_w2", [P, D])
        S.maa_w2g = sb("maa_w2g", [32, D])
        S.Wr, S.Wk, S.Wv, S.Wo = (sb(n, [P, DC, D]) for n in ("Wr", "Wk", "Wv", "Wo"))
        S.gw1 = sb("gw1", [P, DC, N])
        S.gw2 = sb("gw2", [N, D])
        S.dw1 = sb("dw1", [P, DC, N])
        S.dw2 = sb("dw2", [N, D])
        S.ln_g = sb("ln_g", [P, D])
        S.ln_b = sb("ln_b", [P, D])
        chvec, maa_w1, maa_w2, square, gw1, gw2, dw1, dw2, ln_g, ln_b = S.mix_weights
        loads = [(S.ch[:, :, :], chvec), (S.maa_w1[:, :, :], maa_w1), (S.maa_w2[:, :], maa_w2[0:P, :]),
                 (S.maa_w2g[:, :], maa_w2[P:160, :])]
        loads += [(t[:, :, :], w) for t, w in zip((S.Wr, S.Wk, S.Wv, S.Wo), square)]
        loads += [(S.gw1[:, :, :], gw1), (S.gw2[:, :], gw2), (S.dw1[:, :, :], dw1), (S.dw2[:, :], dw2),
                  (S.ln_g[:, :], ln_g.partition_broadcast(P)), (S.ln_b[:, :], ln_b.partition_broadcast(P))]
        xn_ready = sem("xn_ready")
        carry_ready = sem("carry_ready")
        turned = sem("turned")
        xT_ready = sem("xT_ready")
        xxx_ready = sem("xxx_ready")
        mixed = [sem(f"mixed{j}") for j in range(2)]
        tmp_ready = [sem(f"tmp_ready{j}") for j in range(2)]
        kr_ready = sem("kr_ready")
        wl_ready = sem("wl_ready")
        w_ready = sem("w_ready")
        ru_ready = sem("ru_ready")
        v_ready = sem("v_ready")
        g_ready = sem("g_ready")
        prod_ready = [sem(f"prod_ready{r}") for r in range(2)]
        prod_used = [sem(f"prod_used{r}") for r in range(2)]
        level_ready = [sem(f"level_ready{r}") for r in range(2)]
        ks_turned = sem("ks_turned")
        af_ready = sem("af_ready")
        a_zero = sem("a_zero")
        krow_ready = sem("krow_ready")
        state_ready = sem("state_ready")
        y_ready = sem("y_ready")
        yc_ready = sem("yc_ready")
        sq_ready = sem("sq_ready")
        yn_ready = sem("yn_ready")
        yg_ready = sem("yg_ready")
        yg_turned = sem("yg_turned")
        ygT_ready = sem("ygT_ready")
        xx_ready = sem("xx_ready")
        arrive_chain, level_chain, state_chain, norm_chain = (
            sem(n) for n in ("arrive_chain", "level_chain", "state_chain", "norm_chain"))
        achain = sem("mix_scalar_chain")
        pchain = sem("mix_pool_chain")

        LORA, LORAG, M0, DW1, GW1, K0, R0, DW2, V0, G0, ST0, Y0, O0 = 0, 1, 2, 12, 13, 14, 16, 18, 20, 22, 24, 25, 32
        JB = NJ // NBK

        def before(g, j, last=False):
            if j < DW1:
                return j // NBK if isinstance(g, int) and g == 0 else g * JB + (j // NBK - 1)
            if j < O0:
                return g * JB + j // NBK
            return g * JB + (JB - 1 if last else JB + 2)

        def fill(pe, g, j, last=False):
            if due(before(g, j, last)):
                pe.wait_ge(drained[j % NBK], before(g, j, last))
            return B[j % NBK]

        def full(eng, g, j, last=False):
            eng.wait_ge(filled[j % NBK], before(g, j, last) + 1)
            return B[j % NBK]

        def emptied(eng, g, j):
            eng.wait_ge(drained[j % NBK], before(g, j) + 1)

        ARRIVE, LEVEL, NORM = 20, 29, 5

        def ln_roots(G):
            return S.n_roots["mix"] + 1 if isinstance(G, int) and G == 0 else G * 2 + S.n_roots["mix"]

        def gn_roots(g, last):
            return g * 2 + (S.n_roots["mix"] + (2 if last else 3))

        def blocks(a, l):
            return a.rearrange("p (b h s) -> p b h s", h=2, s=1 << l)

        with nc.Block() as block:
            @block.sync
            def _(sp):
                for dst, src in loads:
                    sp.dma_start(dst, src).then_inc(weights_loaded, 16)

            @block.vector
            def _(dve):
                def arrive(G, u, k, turn):
                    c = Chain(dve, arrive_chain, G * ARRIVE + [0, 4, 8, 12, 16, 17][k])
                    if k < 2:
                        if k == 0:
                            if u == 0:
                                dve.memset(xT[:, :, 0:1], 0.0).then_inc(carry_ready, 1)
                            else:
                                dve.tensor_copy(xT[:, :, 0:1], xT[:, :, GT:GT + 1]).then_inc(carry_ready, 1)
                            dve.wait_ge(gathered[u], turn * (16 * GQ * TOPK))
                            dve.tensor_copy(idx[1 - u][:, :, :],
                                            S.gidx[:, bass.ds((G + 1) * GQ, GQ), :]).then_inc(idx_ready, 1)
                        for q in range(GQ):
                            x = S.x_sb[:, G * GQ + q, :]
                            c(dve.scalar_tensor_tensor(out=x, in0=fetched[u][:, q, k, :],
                                                       scalar=S.gw[:, G * GQ + q, k:k + 1],
                                                       in1=x, op0=ALU.mult, op1=ALU.add))
                        c.settle()
                        S.apart(dve)
                    elif k == 2:
                        for q in range(GQ):
                            c(dve.bn_stats(st[:, q, :], S.x_sb[:, G * GQ + q, :]))
                        c.settle()
                        S.apart(dve)
                    elif k == 3:
                        for q in range(GQ):
                            c(dve.bn_aggr(mv[:, q, :], st[:, q, :]))
                        c.settle()
                        dve.sem_inc(S.var_ready, 1)
                    elif k == 4:
                        dve.wait_ge(S.rstd_ready, ln_roots(G))
                        c(dve.reciprocal(rstd[:, :], rstd[:, :]))
                        c.settle()
                    else:
                        for q in range(GQ):
                            t = dve.tensor_scalar(xn[:, q, :], S.x_sb[:, G * GQ + q, :], mv[:, q, 0:1],
                                                  rstd[:, q:q + 1], ALU.subtract, ALU.mult)
                            if q < GQ - 1:
                                c(t)
                        t.then_inc(xn_ready, 1)

                def shift(G):
                    dve.wait_ge(xT_ready, G + 1)
                    dve.tensor_tensor(xx[:, :, :], xT[:, :, 0:GT], xT[:, :, 1:GT + 1], ALU.subtract).then_inc(xx_ready, 1)
                    dve.wait_ge(xx_ready, G + 1)
                    for k in range(DC):
                        t = dve.scalar_tensor_tensor(out=xxx[:, k, :], in0=xx[:, k, :], scalar=S.ch[:, 0, k:k + 1],
                                                     in1=xT[:, k, 1:GT + 1], op0=ALU.mult, op1=ALU.add)
                        t.then_inc(xxx_ready, 1)

                def mix_in(G, j):
                    f, k = j // 2, j % 2
                    b = full(dve, G, M0 + j)
                    if due(G * 5 + f):
                        dve.wait_ge(mixed[k], G * 5 + f)
                    dve.scalar_tensor_tensor(out=tmp[k][:, :], in0=b[:, :], scalar=S.ch[:, 1 + f, k:k + 1],
                                             in1=xx[:, k, :], op0=ALU.add, op1=ALU.mult).then_inc(tmp_ready[k], 1)
                    dve.wait_ge(tmp_ready[k], G * 5 + (f + 1))
                    dve.sem_inc(drained[(M0 + j) % NBK], 1)

                def decay_and_bonus(G):
                    for k in range(DC):
                        b = full(dve, G, DW2 + k)
                        dve.tensor_scalar(tot[1][:, :] if k == 0 else xxx[:, 0, :], b[:, :],
                                          S.ch[:, 6, k:k + 1], 10.0, ALU.add, ALU.min).then_inc(wl_ready, 1)
                        dve.wait_ge(wl_ready, G * 2 + (k + 1))
                        dve.sem_inc(drained[(DW2 + k) % NBK], 1)
                    dve.wait_ge(kr_ready, G * 4 + 4)
                    for k in range(DC):
                        dve.tensor_scalar(RU[:, k, :], RP[:, k, :], S.ch[:, 7, k:k + 1], None,
                                          ALU.mult).then_inc(ru_ready, 1)

                def levels(g, u, i, ahead):
                    c = Chain(dve, level_chain, g * LEVEL)
                    if u == 0:
                        c(dve.memset(Sbd[:, :, :], 0.0))
                    else:
                        c(dve.memset(mean[:, :], 0.0))
                    c.settle()
                    products = [PP[r][:, :, 0:GQ * N].rearrange("p h (q n) -> p h q n", n=N) for r in range(2)]
                    A4 = [A[:, r * 8:(r + 1) * 8, :].rearrange("p (h q) n -> p h q n", h=2) for r in range(2)]
                    for r in range(2):
                        dve.wait_ge(prod_ready[r], g * 8 + 1)
                        dve.tensor_tensor(A4[r], products[r],
                                          S.diag[:, :].unsqueeze(1).unsqueeze(1).to_broadcast([P, 2, GQ, N]),
                                          ALU.mult).then_inc(prod_used[r], 1)
                    dve.wait_ge(w_ready, g * 2 + 2)
                    for l in range(LEVELS):
                        nb = GT >> (l + 1)
                        shape = [P, nb, 1 << l]
                        for r in range(2):
                            dve.wait_ge(prod_ready[r], g * 8 + (l + 2))
                            rp, ks = blocks(RP[:, r, :], l), blocks(KS[:, r, :], l)
                            tl = tot[l][:, r * 2 * nb:(r + 1) * 2 * nb].rearrange("p (b h) -> p b h", h=2)
                            if l:
                                dve.wait_ge(level_ready[r], g * 7 + l)
                            c(dve.tensor_tensor(rp[:, :, 1, :], rp[:, :, 1, :], tl[:, :, 0:1].to_broadcast(shape), ALU.mult))
                            c(dve.tensor_tensor(tot[l + 1][:, r * nb:(r + 1) * nb], tl[:, :, 0], tl[:, :, 1], ALU.mult))
                            dve.tensor_tensor(ks[:, :, 0, :], ks[:, :, 0, :], tl[:, :, 1:2].to_broadcast(shape),
                                              ALU.mult).then_inc(level_ready[r], 1)
                            if l < 6:
                                dve.wait_ge(prod_used[r], g * 7 + (l + 1))
                                S.apart(dve)
                                dve.copy_predicated(
                                    A4[r], S.lev[:, l, :].unsqueeze(1).unsqueeze(1).to_broadcast([P, 2, GQ, N]),
                                    products[r]).then_inc(prod_used[r], 1)
                        if l < 6 and ahead:
                            arrive(g + 1, 1 - u, l, i + (1 + u))
                    c.settle()
                    S.check(c.n, LEVEL, "level steps")

                def state(g):
                    c = Chain(dve, state_chain, g * (4 * GQ))
                    for q in range(GQ):
                        b = full(dve, g, ST0 + 2 * q)
                        full(dve, g, Y0 + 2 * q)
                        bs = b[:, 0:2 * P].rearrange("p (r n) -> p r n", n=P)
                        for r in range(2):
                            for h in range(2):
                                rows = slice(h * N, h * N + N)
                                c(dve.scalar_tensor_tensor(
                                    out=Sbd[rows, r, rows], in0=Sbd[rows, r, rows],
                                    scalar=tot[LEVELS][rows, r * GQ + q:r * GQ + q + 1],
                                    in1=bs[rows, r, rows], op0=ALU.mult, op1=ALU.add))
                        c.settle()
                        dve.sem_inc(state_ready, 1)
                        dve.sem_inc(drained[(ST0 + 2 * q) % NBK], 1)

                yh = lambda t: t[:, :, :].rearrange("p q (h n) -> p (q h) n", n=N)
                bc = lambda t: t[:, :].unsqueeze(2).to_broadcast([P, GQ * H, N])

                def center(g):
                    c = Chain(dve, norm_chain, g * NORM)
                    dve.wait_ge(y_ready, g * GQ + GQ)
                    c(dve.tensor_reduce(mean[:, :], yh(Y), AX.X, ALU.add))
                    c.settle()
                    c(dve.tensor_scalar(mean[:, :], mean[:, :], 1.0 / N, None, ALU.mult))
                    c.settle()
                    dve.tensor_tensor(yh(Y), yh(Y), bc(mean), ALU.subtract).then_inc(yc_ready, 1)

                def variance(g):
                    c = Chain(dve, norm_chain, g * NORM + 2)
                    dve.wait_ge(sq_ready, g + 1)
                    c(dve.tensor_reduce(var[:, :], yh(Y2), AX.X, ALU.add))
                    c.settle()
                    dve.tensor_scalar(var[:, :], var[:, :], 1.0 / N, None, ALU.mult).then_inc(S.var_ready, 1)

                def normalise(g, last):
                    c = Chain(dve, norm_chain, g * NORM + 3)
                    dve.wait_ge(S.rstd_ready, gn_roots(g, last))
                    c(dve.reciprocal(rvar[:, :], rvar[:, :]))
                    c.settle()
                    dve.wait_ge(yc_ready, g + 1)
                    c(dve.tensor_tensor(yh(Y), yh(Y), bc(rvar), ALU.mult))
                    c.settle()
                    dve.tensor_tensor(Y[:, :, :], Y[:, :, :], S.ln_g[:, :].unsqueeze(1).to_broadcast([P, GQ, D]),
                                      ALU.mult).then_inc(yn_ready, 1)

                def add_out(g, last):
                    for q in range(GQ):
                        b = full(dve, g, O0 + q, last)
                        x = S.x_sb[:, g * GQ + q, :]
                        dve.tensor_tensor(x, x, b[:, 0:D], ALU.add).then_inc(drained[(O0 + q) % NBK], 1)

                dve.tensor_copy(idx[0][:, :, :], S.gidx[:, 0:GQ, :]).then_inc(idx_ready, 1)
                for k in range(6):
                    arrive(0, 0, k, 1)
                dve.wait_ge(weights_loaded, 16 * len(loads))
                shift(0)
                for j in range(10):
                    mix_in(0, j)
                decay_and_bonus(0)

                def step(i, last):
                    for u in range(2):
                        g = i * 2 + u
                        end = last and u == 1
                        levels(g, u, i, not end)
                        if not end:
                            shift(g + 1)
                        state(g)
                        center(g)
                        if not end:
                            for j in range(3):
                                mix_in(g + 1, j)
                        variance(g)
                        if not end:
                            for j in range(3, 6):
                                mix_in(g + 1, j)
                        normalise(g, end)
                        if not end:
                            for j in range(6, 10):
                                mix_in(g + 1, j)
                        add_out(g, end)
                        if not end:
                            decay_and_bonus(g + 1)

                loop_with_last(dve, T // SEQ, step)

            @block.gpsimd
            def _(pool):
                def gather(g, u):
                    pool.wait_ge(idx_ready, g + 1)
                    S.apart(pool)
                    for q in range(GQ):
                        for k in range(TOPK):
                            pool.indirect_dma_start(
                                fetched[u][:, q, k, :], None, S.eout[:, :],
                                bass.IndirectOffsetOnAxis(ap=idx[u][:, q, k:k + 1], axis=0)
                            ).then_inc(gathered[u], 16)

                def mix_in(G, j):
                    f, k = j // 2, j % 2
                    pool.wait_ge(tmp_ready[k], G * 5 + (f + 1))
                    pool.tensor_tensor(xf[f][:, k, :], tmp[k][:, :], xT[:, k, 1:GT + 1],
                                       ALU.add).then_inc(mixed[k], 1)

                def gate(g):
                    pool.wait_ge(yn_ready, g + 1)
                    pool.tensor_tensor(Y[:, :, :], Y[:, :, :], S.ln_b[:, :].unsqueeze(1).to_broadcast([P, GQ, D]),
                                       ALU.add).then_inc(pchain, 1)
                    pool.wait_ge(pchain, g + 1)
                    pool.wait_ge(g_ready, g * 2 + 2)
                    pool.tensor_tensor(Y2[:, :, :], Y[:, :, :], G[:, :, :], ALU.mult).then_inc(yg_ready, 1)

                pool.memset(Af[:, :, :], 0.0).then_inc(a_zero, 1)
                gather(0, 0)
                pool.wait_ge(weights_loaded, 16 * len(loads))
                for j in range(10):
                    mix_in(0, j)
                gather(1, 1)

                def step(i, last):
                    for u in range(2):
                        g = i * 2 + u
                        end = last and u == 1
                        if not end:
                            for j in range(6):
                                mix_in(g + 1, j)
                        gate(g)
                        if not end:
                            for j in range(6, 10):
                                mix_in(g + 1, j)
                            gather(g + 2, u)

                loop_with_last(pool, T // SEQ, step)
                pool.wait_ge(gathered[0], (T // SEQ + 1) * 16 * GQ * TOPK)

            @block.scalar
            def _(act):
                def arrive(G):
                    root(act, S, mv[:, :, 1], S.eps[:, 0:1], rstd[:, :], ln_roots(G))

                def turn_in(G):
                    act.wait_ge(turned, G + 1)
                    act.wait_ge(carry_ready, G + 1)
                    act.copy(xT[:, :, 1:GT + 1], PX[:, :, :]).then_inc(xT_ready, 1)

                def low(G):
                    b = full(act, G, LORA)
                    act.activation(lora[:, :], b[:, :], ACT.Tanh).then_inc(drained[LORA % NBK], 1)
                    b = full(act, G, LORAG)
                    act.activation(lorag[:, :], b[0:32, :], ACT.Tanh).then_inc(drained[LORAG % NBK], 1)

                def projections(g):
                    b = full(act, g, DW1)
                    act.activation(tw[:, :], b[0:N, :], ACT.Tanh).then_inc(drained[DW1 % NBK], 1)
                    b = full(act, g, GW1)
                    act.activation(tg[:, :], b[0:N, :], ACT.Tanh).then_inc(drained[GW1 % NBK], 1)
                    for j, t in ((K0, KS), (R0, RP)):
                        for k in range(DC):
                            b = full(act, g, j + k)
                            act.copy(t[:, k, :], b[:, :]).then_inc(drained[(j + k) % NBK], 1)
                            emptied(act, g, j + k)
                            act.sem_inc(kr_ready, 1)
                    rate = [Y2[:, 0:2, :].rearrange("p a b -> p (a b)"), xxx[:, 1, :]]
                    for k in range(DC):
                        act.wait_ge(wl_ready, g * 2 + (k + 1))
                        act.activation(rate[k], tot[1][:, :] if k == 0 else xxx[:, 0, :], ACT.Exp).then_inc(achain, 1)
                    act.wait_ge(achain, g * 2 + 2)
                    for k in range(DC):
                        act.activation(W[:, k * GT:(k + 1) * GT], rate[k], ACT.Exp, scale=-1.0).then_inc(w_ready, 1)
                    for j, t in ((V0, V), (G0, G)):
                        for k in range(2):
                            b = full(act, g, j + k)
                            act.copy(t[:, 2 * k:2 * k + 2, :],
                                     b[:, :].rearrange("p (q d) -> p q d", d=D)).then_inc(drained[(j + k) % NBK], 1)
                            emptied(act, g, j + k)
                            act.sem_inc(v_ready if t is V else g_ready, 1)

                def assemble(g):
                    act.wait_ge(a_zero, 1)
                    for r in range(2):
                        act.wait_ge(prod_ready[r], g * 8 + 8)
                        act.copy(Af[0:N, r * 8:(r + 1) * 8, N:P].rearrange("p (h q) n -> p h q n", h=2),
                                 PP[r][0:N, :, 0:GQ * N].rearrange("p h (q n) -> p h q n", n=N)).then_inc(af_ready, 1)
                        act.wait_ge(prod_used[r], g * 7 + 7)
                    act.copy(Af[0:N, :, 0:N], A[0:N, :, :]).then_inc(af_ready, 1)
                    act.copy(Af[N:P, :, N:P], A[N:P, :, :]).then_inc(af_ready, 1)

                def key_rows(g):
                    act.wait_ge(ks_turned, g + 1)
                    act.copy(KR[:, :, :].rearrange("p (a q) d -> p a (q d)", a=2), PA[:, :, :]
                             ).then_inc(krow_ready, 1)

                def outputs(g):
                    for q in range(GQ):
                        b = full(act, g, Y0 + 2 * q)
                        act.copy(Y[:, q, :], b[:, 0:D]).then_inc(drained[(Y0 + 2 * q) % NBK], 1)
                        emptied(act, g, Y0 + 2 * q)
                        act.sem_inc(y_ready, 1)

                def squares(g, last):
                    act.wait_ge(yc_ready, g + 1)
                    act.activation(Y2[:, :, :], Y[:, :, :], ACT.Square).then_inc(sq_ready, 1)
                    root(act, S, var[:, :], S.eps[:, 1:2], rvar[:, :], gn_roots(g, last))

                def gated(g):
                    act.wait_ge(yg_turned, g + 1)
                    act.copy(ygT[:, :, :], PA[:, :, :]).then_inc(ygT_ready, 1)

                arrive(0)
                turn_in(0)
                low(0)
                projections(0)

                def step(i, last):
                    for u in range(2):
                        g = i * 2 + u
                        end = last and u == 1
                        if not end:
                            arrive(g + 1)
                        assemble(g)
                        if not end:
                            turn_in(g + 1)
                        key_rows(g)
                        outputs(g)
                        if not end:
                            low(g + 1)
                        squares(g, end)
                        gated(g)
                        if not end:
                            projections(g + 1)

                loop_with_last(act, T // SEQ, step)

            @block.tensor
            def _(pe):
                pairs = [(r, h) for r in range(2) for h in range(2)]

                def halves(r, ks, rp):
                    for q in range(GQ):
                        for c in range(2):
                            ts = slice(q * P + c * N, q * P + c * N + N)
                            for h in range(2):
                                rows = slice(h * N, h * N + N)
                                t = pe.matmul(PP[r][c * N:c * N + N, h, q * N:(q + 1) * N],
                                              ks[rows, r, ts], rp[rows, r, ts], start=True, stop=True,
                                              skip_group_check=True)
                    t.then_inc(prod_ready[r], 1)

                def turn_in(G):
                    pe.wait_ge(xn_ready, G + 1)
                    if due(G * 4 - 3):
                        pe.wait_ge(af_ready, G * 4 - 3)
                    for q in range(GQ):
                        for k in range(DC):
                            t = pe.transpose(PX[:, k, q * P:(q + 1) * P], xn[:, q, k * P:(k + 1) * P], S.ident[:, :])
                    t.then_inc(turned, 1)

                def low(g):
                    pe.wait_ge(xxx_ready, g * 2 + 2)
                    for j, n, o in ((LORA, P, 0), (LORAG, 32, P)):
                        b = fill(pe, g, j)
                        for k in range(DC):
                            t = pe.matmul(b[0:n, :], S.maa_w1[:, k, o:o + n], xxx[:, k, :], start=(k == 0), stop=(k == 1))
                        t.then_inc(filled[j % NBK], 1)
                    emptied(pe, g, LORA)
                    emptied(pe, g, LORAG)
                    for j in range(10):
                        f, k = j // 2, j % 2
                        b = fill(pe, g, M0 + j)
                        if f < 4:
                            t = pe.matmul(b[:, :], S.maa_w2[32 * f:32 * f + 32, k * P:(k + 1) * P],
                                          lora[32 * f:32 * f + 32, :], start=True, stop=True,
                                          tile_position=(32 * f, 0))
                        else:
                            t = pe.matmul(b[:, :], S.maa_w2g[:, k * P:(k + 1) * P], lorag[:, :],
                                          start=True, stop=True)
                        t.then_inc(filled[(M0 + j) % NBK], 1)

                def projections(g):
                    def mixed_in(f):
                        for k in range(DC):
                            pe.wait_ge(mixed[k], g * 5 + (f + 1))

                    def project(j, w, x, n=P, o=0):
                        b = fill(pe, g, j)
                        for k in range(DC):
                            t = pe.matmul(b[0:n, :], w[:, k, o:o + n], x[:, k, :], start=(k == 0), stop=(k == 1))
                        t.then_inc(filled[j % NBK], 1)

                    mixed_in(0)
                    project(DW1, S.dw1, xf[0], N)
                    mixed_in(4)
                    project(GW1, S.gw1, xf[4], N)
                    for k in range(DC):
                        project(K0 + k, S.Wk, xf[1], P, k * P)
                    for k in range(DC):
                        project(R0 + k, S.Wr, xf[3], P, k * P)
                    emptied(pe, g, DW1)
                    for k in range(DC):
                        b = fill(pe, g, DW2 + k)
                        pe.matmul(b[:, :], S.dw2[:, k * P:(k + 1) * P], tw[:, :], start=True,
                                  stop=True).then_inc(filled[(DW2 + k) % NBK], 1)
                    for a in range(2):
                        b = fill(pe, g, V0 + a)
                        for q in range(2):
                            for k in range(DC):
                                s = (2 * a + q) * P
                                t = pe.matmul(b[:, q * D:(q + 1) * D], xf[2][:, k, s:s + P], S.Wv[:, k, :],
                                              start=(k == 0), stop=(k == 1))
                        t.then_inc(filled[(V0 + a) % NBK], 1)
                    emptied(pe, g, GW1)
                    for a in range(2):
                        b = fill(pe, g, G0 + a)
                        for q in range(2):
                            s = (2 * a + q) * P
                            t = pe.matmul(b[:, q * D:(q + 1) * D], tg[:, s:s + P], S.gw2[:, :], start=True, stop=True)
                        t.then_inc(filled[(G0 + a) % NBK], 1)

                def levels(g):
                    pe.wait_ge(kr_ready, g * 4 + 4)
                    for r in range(2):
                        pe.wait_ge(ru_ready, g * 2 + (r + 1))
                        S.apart(pe)
                        halves(r, KS, RU)
                    for l in range(7):
                        for r in range(2):
                            if l:
                                pe.wait_ge(level_ready[r], g * 7 + l)
                            pe.wait_ge(prod_used[r], g * 7 + (l + 1))
                            S.apart(pe)
                            if l < 6:
                                halves(r, KS, RP)
                                continue
                            for q in range(GQ):
                                for h in range(2):
                                    rows = slice(h * N, h * N + N)
                                    t = pe.matmul(PP[r][0:N, h, q * N:(q + 1) * N],
                                                  KS[rows, r, q * P:q * P + N], RP[rows, r, q * P + N:(q + 1) * P],
                                                  start=True, stop=True, skip_group_check=True)
                            t.then_inc(prod_ready[r], 1)

                def key_rows(g):
                    for r in range(2):
                        pe.wait_ge(level_ready[r], g * 7 + 7)
                    pe.wait_ge(af_ready, g * 4 + 2)
                    for q in range(GQ):
                        for r in range(2):
                            t = pe.transpose(PA[:, q // 2, (q % 2) * D + r * P:(q % 2) * D + (r + 1) * P],
                                             KS[:, r, q * P:(q + 1) * P], S.ident[:, :])
                    t.then_inc(ks_turned, 1)

                def state_and_y(g):
                    pe.wait_ge(krow_ready, g + 1)
                    pe.wait_ge(v_ready, g * 2 + 2)
                    pe.wait_ge(af_ready, g * 4 + 4)
                    for q in range(GQ):
                        b = fill(pe, g, ST0 + 2 * q)
                        for r in range(2):
                            rs = slice(r * P, (r + 1) * P)
                            t = pe.matmul(b[:, rs], KR[:, q, rs], V[:, q, rs], start=True, stop=True)
                        t.then_inc(filled[(ST0 + 2 * q) % NBK], 1)
                        b = fill(pe, g, Y0 + 2 * q)
                        for r, h in pairs:
                            cs = slice(r * P + h * N, r * P + h * N + N)
                            pe.matmul(b[:, cs], Af[:, (r * 2 + h) * GQ + q, :], V[:, q, cs], start=(r == 0 and h == 0),
                                      stop=False, skip_group_check=True)
                        if due(g * GQ + q):
                            pe.wait_ge(state_ready, g * GQ + q)
                        for r in range(2):
                            rs = slice(r * P, (r + 1) * P)
                            t = pe.matmul(b[:, rs], RP[:, r, q * P:(q + 1) * P], Sbd[:, r, :], start=False,
                                          stop=(r == 1), skip_group_check=True)
                        t.then_inc(filled[(Y0 + 2 * q) % NBK], 1)

                def output(g, last):
                    pe.wait_ge(yg_ready, g + 1)
                    for q in range(GQ):
                        for k in range(DC):
                            t = pe.transpose(PA[:, k, q * P:(q + 1) * P], Y2[:, q, k * P:(k + 1) * P], S.ident[:, :])
                    t.then_inc(yg_turned, 1)
                    pe.wait_ge(ygT_ready, g + 1)
                    for q in range(GQ):
                        b = fill(pe, g, O0 + q, last)
                        for k in range(DC):
                            t = pe.matmul(b[:, 0:D], ygT[:, k, q * P:(q + 1) * P], S.Wo[:, k, :],
                                          start=(k == 0), stop=(k == 1))
                        t.then_inc(filled[(O0 + q) % NBK], 1)

                turn_in(0)
                pe.wait_ge(weights_loaded, 16 * len(loads))
                low(0)
                projections(0)

                def step(i, last):
                    for u in range(2):
                        g = i * 2 + u
                        end = last and u == 1
                        levels(g)
                        if not end:
                            turn_in(g + 1)
                        key_rows(g)
                        state_and_y(g)
                        if not end:
                            low(g + 1)
                        output(g, end)
                        if not end:
                            projections(g + 1)

                loop_with_last(pe, T // SEQ, step)


class Shared:

    def __init__(self, nc, ctx):
        self.nc, self.ctx, self.stage_sems = nc, ctx, []

    def sem(self, name):
        s = self.nc.alloc_semaphore(name=name)
        self.stage_sems.append(s)
        return s

    def keep(self):
        self.stage_sems = []

    def end_stage(self):
        self.nc.clear_and_free_semaphores(self.stage_sems)
        self.nc.all_engine_barrier()
        self.stage_sems = []

    def apart(self, eng):
        eng.sem_inc(self.passed, 1)

    def check(self, n, want, what):
        assert n == want, (what, n, want)


def program(nc, x, rwT, rb, w1, b1T, w2, b2, chvec, maa_w1, maa_w2, Wr, Wk, Wv, Wo, gw1, gw2, dw1, dw2,
            ln_g, ln_b, out):
    with ExitStack() as ctx:
        S = Shared(nc, ctx)

        def sb(name, shape, dt=F32):
            return ctx.enter_context(nc.sbuf_tensor(name, shape, dt))

        S.var_ready = S.sem("var_ready")
        S.rstd_ready = S.sem("rstd_ready")
        S.passed = S.sem("passed")
        S.slots_zeroed = S.sem("slots_zeroed")
        S.n_roots = {"a": 0, "mix": NG, "b": 3 * NG}
        S.x, S.w1, S.w2, S.out = x, w1, w2, out
        S.slots = nc.dram_tensor("slots", [E * CAP, D], F32, kind="Internal").ap()
        S.eout = nc.dram_tensor("eout", [E * CAP, D], F32, kind="Internal").ap()
        S.keep()
        S.x_sb = sb("x_sb", [P, NT, D])
        S.gidx = sb("gidx", [P, NT + GQ, TOPK], U32)
        S.gw = sb("gw", [P, NT, TOPK])
        S.b1 = sb("b1", [P, E * FC])
        S.b2 = b2
        S.rb = sb("rb", [P, E])
        S.rwT = sb("rwT", [P, DC, E])
        S.eps = sb("eps", [P, 2])
        S.ident = sb("ident", [P, P])
        S.before = sb("before", [P, P])
        S.ones = sb("ones", [P, P])
        S.iota_i = sb("iota_i", [P, E], mybir.dt.int32)
        S.iota_f = sb("iota_f", [P, E])
        rows = lambda w: w.rearrange("(c p) n -> p c n", p=P)
        S.loads = [(S.b1[:, :], b1T), (S.rb[:, :], rb.partition_broadcast(P)), (S.rwT[:, :, :], rows(rwT))]
        S.mix_weights = (chvec, rows(maa_w1), maa_w2, [rows(w) for w in (Wr, Wk, Wv, Wo)], rows(gw1), gw2,
                         rows(dw1), dw2, ln_g, ln_b)
        with nc.sbuf_tensor("zeros", [P, 2560], F32) as zeros:
            S.zeros = zeros
            constants(nc, S)
            S.end_stage()
            for tag in "ab":
                route(nc, S, tag)
                S.end_stage()
                experts(nc, S, tag)
                S.end_stage()
                if tag == "a":
                    mix(nc, S)
                    S.end_stage()
            combine(nc, S, tag)


def kernel(**inputs):
    import numpy as np
    import concourse.bacc as bacc
    from concourse.bass_utils import run_bass_kernel_spmd

    f = lambda k: np.asarray(inputs[k])
    att = lambda k: f("L0_attn_" + k)
    ffn = lambda k: f("L0_ffn_" + k)
    vectors = [att("maa_x"), att("maa_w"), att("maa_k"), att("maa_v"), att("maa_r"), att("maa_g"),
               att("time_decay"), att("u").reshape(-1)]
    arrays = {
        "x": att("x").reshape(T, D),
        "rwT": ffn("router_w").T,
        "rb": ffn("router_b"),
        "w1": ffn("w1"),
        "b1T": ffn("b1").reshape(E, FC, P).transpose(2, 0, 1).reshape(P, E * FC),
        "w2": ffn("w2"),
        "b2": ffn("b2"),
        "chvec": np.stack(vectors).reshape(8, DC, P).transpose(2, 0, 1),
        "maa_w1": att("maa_w1"),
        "maa_w2": att("maa_w2").reshape(160, D),
        "Wr": att("Wr"), "Wk": att("Wk"), "Wv": att("Wv"), "Wo": att("Wo"),
        "gw1": att("gate_w1"), "gw2": att("gate_w2"), "dw1": att("decay_w1"), "dw2": att("decay_w2"),
        "ln_g": att("ln_g"), "ln_b": att("ln_b"),
    }
    arrays = {"in_" + k: np.ascontiguousarray(a) for k, a in arrays.items()}
    nc = bacc.Bacc("TRN2", target_bir_lowering=False, num_devices=1)
    args = [nc.dram_tensor(k, a.shape, mybir.dt.from_np(a.dtype), kind="ExternalInput").ap()
            for k, a in arrays.items()]
    out = nc.dram_tensor("out", (T, D), F32, kind="ExternalOutput").ap()
    program(nc, *args, out)
    r = run_bass_kernel_spmd(nc, [arrays], core_ids=[0])
    return r.results[0]["out"].reshape(T // SEQ, SEQ, D)
```
